# Optimizing a Trainium2 kernel written in Bass

```python
import numpy as np
import jax
import jax.numpy as jnp

def _softmax(x, axis=-1):
    return jax.nn.softmax(x, axis=axis)

def _gelu(x):
    return jax.nn.gelu(x, approximate=True)

def _silu(x):
    return jax.nn.silu(x)

def _sigmoid(x):
    return jax.nn.sigmoid(x)

def _layernorm(x, axis=-1, eps=1e-05):
    m = jnp.mean(x, axis=axis, keepdims=True)
    v = jnp.var(x, axis=axis, keepdims=True)
    return (x - m) / jnp.sqrt(v + eps)

def _scatter_add(tgt, idx, src, axis=0):
    return tgt.at[idx].add(src)

def _segment_sum(src, seg, n):
    return jax.ops.segment_sum(src, seg, n)
kernel_name = 'mk_gnn_resnorm_d2_gnn_r64_92fd05'

def setup_inputs(seed: int=0):
    np.random.seed(seed)
    _w = jnp.asarray

    def _rec_inputs():
        import jax
        import jax.numpy as jnp
        _gk = jax.random.key(seed)
        x = -0.000202 + 1 * jax.random.normal(jax.random.fold_in(_gk, 1), (100000, 64), jnp.float32)
        src = jax.random.randint(jax.random.fold_in(_gk, 2), (50000,), 0, 100000, jnp.int32)
        dst = jax.random.randint(jax.random.fold_in(_gk, 3), (50000,), 0, 100000, jnp.int32)
        _o = jnp.argsort(dst, stable=True)
        src = src[_o]
        dst = dst[_o]
        edge_weight = jax.random.uniform(jax.random.fold_in(_gk, 13), (50000,), jnp.float32, 0.0, 0.999999)
        return (x, src, dst, edge_weight)
    x, src, dst, edge_weight = _rec_inputs()

    def _L0_gnn_setup():
        import jax, jax.numpy as jnp
        import numpy as np
        N_NODES = 100000
        N_EDGES = 1250000
        D_FEAT = 64
        D_OUT = 64
        LEAKY_ALPHA = 0.2
        L2_EPS = 1e-12
        key = jax.random.key(seed)
        ks = jax.random.split(key, 8)
        features = jax.random.normal(ks[0], (N_NODES, D_FEAT), dtype=jnp.float32)
        src = jax.random.randint(ks[1], (N_EDGES,), 0, N_NODES, dtype=jnp.int32)
        dst = jax.random.randint(ks[2], (N_EDGES,), 0, N_NODES, dtype=jnp.int32)
        edge_weight = jax.random.uniform(ks[3], (N_EDGES,), dtype=jnp.float32)
        scale = 1.0 / np.sqrt(D_FEAT)
        W1 = jax.random.normal(ks[4], (D_FEAT, D_OUT), dtype=jnp.float32) * scale
        W2 = jax.random.normal(ks[5], (D_FEAT, D_OUT), dtype=jnp.float32) * scale
        b1 = jax.random.normal(ks[6], (1, D_OUT), dtype=jnp.float32) * scale
        b2 = jax.random.normal(ks[7], (1, D_OUT), dtype=jnp.float32) * scale
        return {'features': features, 'src': src, 'dst': dst, 'edge_weight': edge_weight, 'W1': W1, 'W2': W2, 'b1': b1, 'b2': b2}
    _L0_gnn_all = _L0_gnn_setup()
    _L0_gnn_in = {k: v for k, v in _L0_gnn_all.items() if k in ('W1', 'W2', 'b1', 'b2')}
    del _L0_gnn_all

    def _L1_gnn_setup():
        import jax, jax.numpy as jnp
        import numpy as np
        EPS_L2 = 1e-12

        def _ffn(h, W1, b1, W2, b2):
            h = jax.nn.gelu(h @ W1 + b1, approximate=False)
            h = jax.nn.gelu(h @ W2 + b2, approximate=False)
            return h
        key = jax.random.key(seed)
        ks = jax.random.split(key, 8)
        N, E, D = (50000, 15625, 64)
        x = jax.random.normal(ks[0], (N, D), dtype=jnp.float32)
        edges = jax.random.randint(ks[1], (2, E), 0, N, dtype=jnp.int32)
        edge_weights = jax.random.uniform(ks[2], (E,), dtype=jnp.float32)
        s = 1.0 / np.sqrt(D)
        W1p = jax.random.normal(ks[3], (D, D), dtype=jnp.float32) * s
        b1p = jnp.zeros((D,), jnp.float32)
        W2p = jax.random.normal(ks[4], (D, D), dtype=jnp.float32) * s
        b2p = jnp.zeros((D,), jnp.float32)
        W1u = jax.random.normal(ks[5], (2 * D, D), dtype=jnp.float32) * (1.0 / np.sqrt(2 * D))
        b1u = jnp.zeros((D,), jnp.float32)
        W2u = jax.random.normal(ks[6], (D, D), dtype=jnp.float32) * s
        b2u = jnp.zeros((D,), jnp.float32)
        return {'x': x, 'edges': edges, 'edge_weights': edge_weights, 'W1p': W1p, 'b1p': b1p, 'W2p': W2p, 'b2p': b2p, 'W1u': W1u, 'b1u': b1u, 'W2u': W2u, 'b2u': b2u}
    _L1_gnn_all = _L1_gnn_setup()
    _L1_gnn_in = {k: v for k, v in _L1_gnn_all.items() if k in ('W1p', 'b1p', 'W2p', 'b2p', 'W1u', 'b1u', 'W2u', 'b2u')}
    del _L1_gnn_all
    return {'x': x, 'src': src, 'dst': dst, 'edge_weight': edge_weight, 'L0_gnn_W1': _L0_gnn_in['W1'], 'L0_gnn_W2': _L0_gnn_in['W2'], 'L0_gnn_b1': _L0_gnn_in['b1'], 'L0_gnn_b2': _L0_gnn_in['b2'], 'L1_gnn_W1p': _L1_gnn_in['W1p'], 'L1_gnn_b1p': _L1_gnn_in['b1p'], 'L1_gnn_W2p': _L1_gnn_in['W2p'], 'L1_gnn_b2p': _L1_gnn_in['b2p'], 'L1_gnn_W1u': _L1_gnn_in['W1u'], 'L1_gnn_b1u': _L1_gnn_in['b1u'], 'L1_gnn_W2u': _L1_gnn_in['W2u'], 'L1_gnn_b2u': _L1_gnn_in['b2u']}

def reference(x, src, dst, edge_weight, L0_gnn_W1, L0_gnn_W2, L0_gnn_b1, L0_gnn_b2, L1_gnn_W1p, L1_gnn_b1p, L1_gnn_W2p, L1_gnn_b2p, L1_gnn_W1u, L1_gnn_b1u, L1_gnn_W2u, L1_gnn_b2u):
    import jax
    import jax.numpy as jnp

    def _L0_gnn_ref(features, src, dst, edge_weight, W1, W2, b1, b2):
        import jax, jax.numpy as jnp
        import numpy as np
        N_NODES = 100000
        N_EDGES = 1250000
        D_FEAT = 64
        D_OUT = 64
        LEAKY_ALPHA = 0.2
        L2_EPS = 1e-12
        messages = features[src] * edge_weight[:, None]
        aggregated = jax.ops.segment_sum(messages, dst, num_segments=N_NODES)
        act = lambda x: jax.nn.leaky_relu(x, negative_slope=LEAKY_ALPHA)
        out = act(features * aggregated @ W1 + b1) + act(aggregated @ W2 + b2)
        sq = jnp.sum(out * out, axis=1, keepdims=True)
        return out * jax.lax.rsqrt(jnp.maximum(sq, L2_EPS))

    def _L1_gnn_ref(x, edges, edge_weights, W1p, b1p, W2p, b2p, W1u, b1u, W2u, b2u):
        import jax, jax.numpy as jnp
        import numpy as np
        EPS_L2 = 1e-12

        def _ffn(h, W1, b1, W2, b2):
            h = jax.nn.gelu(h @ W1 + b1, approximate=False)
            h = jax.nn.gelu(h @ W2 + b2, approximate=False)
            return h
        num_nodes = x.shape[0]
        node_indices, neighbour_indices = (edges[0], edges[1])
        nbr = x[neighbour_indices]
        messages = _ffn(nbr, W1p, b1p, W2p, b2p) * edge_weights[:, None]
        agg = jax.ops.segment_sum(messages, node_indices, num_segments=num_nodes)
        h = jnp.concatenate([x, agg], axis=1)
        out = _ffn(h, W1u, b1u, W2u, b2u)
        sq = jnp.sum(out * out, axis=-1, keepdims=True)
        out = out * jax.lax.rsqrt(jnp.maximum(sq, EPS_L2))
        return out
    edge_index = jnp.stack([src, dst])
    x = _layernorm(x + _L0_gnn_ref(x, src, dst, edge_weight, L0_gnn_W1, L0_gnn_W2, L0_gnn_b1, L0_gnn_b2), axis=-1)
    x = _layernorm(x + _L1_gnn_ref(x, edge_index, edge_weight, L1_gnn_W1p, L1_gnn_b1p, L1_gnn_W2p, L1_gnn_b2p, L1_gnn_W1u, L1_gnn_b1u, L1_gnn_W2u, L1_gnn_b2u), axis=-1)
    return x

_drawn_inputs = setup_inputs


def setup_inputs(seed=0):
    import zlib

    import numpy as np

    out = dict(_drawn_inputs(seed))
    spreads = {'L1_gnn_b1p': (0.0, 2.0),
     'L1_gnn_b2p': (0.0, 2.0),
     'L1_gnn_b1u': (0.0, 0.444),
     'L1_gnn_b2u': (0.0, 0.316)}
    factors = {'L1_gnn_W1p': 3.472, 'L1_gnn_W2p': 3.193}
    for name, (base, spread) in spreads.items():
        noise = np.random.default_rng([zlib.crc32(name.encode()), seed]).standard_normal(out[name].shape)
        drawn = base * np.exp(spread * noise) if base else spread * noise
        out[name] = jnp.asarray(drawn.astype(out[name].dtype))
    for name, factor in factors.items():
        out[name] = (out[name] * factor).astype(out[name].dtype)
    return out
```

```python
import numpy as np
import concourse.bass as bass
from concourse import mybir
from contextlib import ExitStack

F32 = mybir.dt.float32
BF16 = mybir.dt.bfloat16
I32 = mybir.dt.int32
ALU = mybir.AluOpType
ACT = mybir.ActivationFunctionType
AX_X = mybir.AxisListType.X

P = 128
D = 64
WT = 4
WE = WT * P
G = 8
CR = P * G
FW = G * D
GH = G // 2
L2_EPS = 1e-12
LN_EPS = 1e-5
SLOPE = 0.2


class Turns:

    def __init__(self, eng, per, j=None, counts=(), laps=()):
        self.eng, self.per, self.j = eng, per, j
        if j is not None:
            self.count = {k: eng.snap(j * per + (k + 1)) for k in counts}
            self.lap = {(n, times): eng.snap(j * times + n * times) for n, times in laps}

    def wait(self, sem, k):
        if self.j is not None:
            self.eng.wait_ge(sem, self.count[k])
        elif k >= 0:
            self.eng.wait_ge(sem, k + 1)

    def wait_slot(self, sems, k, times):
        n = k // self.per + 1
        if self.j is not None:
            self.eng.wait_ge(sems[k % self.per], self.lap[n, times])
        elif n > 0:
            self.eng.wait_ge(sems[k % self.per], n * times)

    def at(self, k, size):
        return k * size if self.j is None else self.eng.snap(self.j * (self.per * size) + k * size)


def run_turns(eng, per, first, start, turns, last, body, counts=(), laps=()):
    for k in range(first, start):
        body(Turns(eng, per), k)
    with eng.Fori(0, turns) as j:
        t = Turns(eng, per, j, counts, laps)
        for k in range(start, start + per):
            body(t, k)
    for k in range(start + turns * per, last + 1):
        body(Turns(eng, per), k)


def gnn_kernel(nc, x, src, dst, edge_weight, w1a, w2a, b1a, b2a, w1p, b1p, w2p, b2p, w1u, b1u, w2u, b2u, out):
    N = x.shape[0]
    E = src.shape[0]
    EC = E // P
    ER = E - EC * P
    NWIN = 2 * -(-E // (2 * WE))
    TILES = NWIN * WT
    assert TILES > EC
    NCH = -(-N // CR)
    TAIL = N - (NCH - 1) * CR
    TG = next(g for g in range(G, 0, -1) if TAIL % g == 0 and TAIL // g <= P)
    TP = TAIL // TG
    TRASH = N + 1
    AROWS = P * -(-(TRASH + WE) // P)
    ZC = AROWS // P * D
    ZPARTS = next(z for z in range(6, 100) if ZC % z == 0)

    x1 = nc.dram_tensor("x1", (N, D), F32, kind="Internal").ap()
    agg = [nc.dram_tensor(f"agg{n}", (AROWS, D), F32, kind="Internal").ap() for n in range(2)]

    ctx = ExitStack()
    with ctx:
        def sb(name, shape, dt=F32, c=ctx):
            return c.enter_context(nc.sbuf_tensor(name, shape, dt))

        def pb(name, c):
            return c.enter_context(nc.psum_tensor(name, [P, 512], F32))

        def sem(name, c=ctx):
            return c.enter_context(nc.semaphore(name))

        gather_idx = [sb(f"gather_idx{n}", [P, TILES], I32) for n in range(2)]
        scatter_raw = [sb(f"scatter_raw{n}", [P, TILES], I32) for n in range(2)]
        ew = sb("ew", [P, TILES])
        sw = [sb(f"sw{n}", [P, NWIN, 2 * WT]) for n in range(2)]
        ident = sb("ident", [P, P])
        earlier = sb("earlier", [P, P])
        earlier_b = sb("earlier_b", [P, P], BF16)
        trash_i = sb("trash_i", [P, WT], I32)
        trash = sb("trash", [P, WT])
        ones3 = sb("ones3", [P, P], BF16)
        wz = sb("wz", [P, 3 * D])
        wp1 = sb("wp1", [P, P])
        wp2 = sb("wp2", [P, P])
        wu1 = sb("wu1", [P, D])
        wu2 = sb("wu2", [P, P])
        bp1 = sb("bp1", [P, 1])
        bu1 = sb("bu1", [P, 1])
        NB0, NB1, NB2 = 2 * 3 * D, WT * D, G * D
        NB = NB0 + NB1 + NB2
        brow = sb("brow", [1, NB])
        brest = sb("brest", [1, NB])
        bparts = sb("bparts", [1, 3, NB], BF16)
        bias = sb("bias", [P, NB], BF16)
        bias0, bias1, bias2 = bias[:, 0:NB0], bias[:, NB0:NB0 + NB1], bias[:, NB0 + NB1:NB]
        zeros = sb("zeros", [P, ZC // ZPARTS])

        loaded = sem("loaded")
        prepared = sem("prepared")
        made = sem("made")
        chain = sem("chain")
        split_done = sem("split_done")
        zeroed = [sem(f"zeroed{n}") for n in range(2)]

        with nc.Block() as block:
            loads = []
            for t, pad, s in ((gather_idx[0], 0, src), (gather_idx[1], 0, dst),
                              (scatter_raw[0], N, dst), (scatter_raw[1], N, src), (ew, 0, edge_weight)):
                loads.append((t[:, 0:EC], s[0:EC * P].rearrange("(p t) -> p t", p=P)))
                if ER:
                    loads.append((t[0:ER, EC:EC + 1], s[EC * P:E].rearrange("(p t) -> p t", t=1)))
            for t, w in ((wp1, w1p), (wp2, w2p), (wu2, w2u)):
                loads += [(t[0:D, 0:D], w), (t[D:2 * D, D:2 * D], w)]
            loads += [(wz[0:D, 0:D], w1a), (wz[D:2 * D, D:2 * D], w2a),
                      (wz[0:D, 2 * D:3 * D], w1a), (wz[D:2 * D, 2 * D:3 * D], w2a), (wu1[:, :], w1u)]
            for t, b in ((bp1, b1p), (bu1, b1u)):
                for h in range(2):
                    loads.append((t[h * D:(h + 1) * D, 0:1], b.rearrange("(f o) -> f o", o=1)))
            for h in range(2):
                loads += [(brow[0:1, (3 * h) * D:(3 * h + 1) * D], b1a), (brow[0:1, (3 * h + 1) * D:(3 * h + 2) * D], b2a)]
            for g in range(WT):
                loads.append((brow[0:1, NB0 + g * D:NB0 + (g + 1) * D], b2p.rearrange("(o f) -> o f", o=1)))
            for g in range(G):
                loads.append((brow[0:1, NB0 + NB1 + g * D:NB0 + NB1 + (g + 1) * D], b2u.rearrange("(o f) -> o f", o=1)))
            N_LOADS = 16 * len(loads)

            @block.vector
            def _(dve):
                for t, pad in ((gather_idx[0], 0), (gather_idx[1], 0), (scatter_raw[0], N), (scatter_raw[1], N)):
                    dve.memset(t[:, EC:TILES], pad)
                dve.memset(ew[:, EC:TILES], 0.0)
                for t in (wp1, wp2, wu2, wz):
                    dve.memset(t[:, :], 0.0)
                dve.memset(bias[:, :], 0.0)
                dve.memset(ones3[:, :], 0.0).then_inc(prepared, 1)
                dve.memset(zeros[:, :], 0.0).then_inc(prepared, 1)
                dve.wait_ge(prepared, 2)
                dve.memset(ones3[0:3, :], 1.0)
                dve.wait_ge(loaded, N_LOADS)
                for n in range(2):
                    dve.tensor_copy(sw[n][:, :, 0:WT], scatter_raw[n][:, :].rearrange("p (k b) -> p k b", b=WT))
                    dve.tensor_copy(sw[n][:, :, WT:2 * WT], ew[:, :].rearrange("p (k b) -> p k b", b=WT))
                dve.tensor_scalar(wz[:, 2 * D:3 * D], wz[:, 2 * D:3 * D], SLOPE, None, ALU.mult)
                b0 = brow[0:1, 0:NB0].rearrange("o (h k f) -> o h k f", h=2, k=3)
                step = 0

                def link(ins):
                    nonlocal step
                    step += 1
                    ins.then_inc(chain, 1)
                    dve.wait_ge(chain, step)

                link(dve.tensor_tensor(b0[:, :, 2, :], b0[:, :, 0, :], b0[:, :, 1, :], ALU.add))
                link(dve.tensor_scalar(b0[:, :, 2, :], b0[:, :, 2, :], SLOPE, None, ALU.mult))
                link(dve.tensor_copy(bparts[0:1, 0, :], brow[0:1, :]))
                link(dve.tensor_tensor(brest[0:1, :], brow[0:1, :], bparts[0:1, 0, :], ALU.subtract))
                link(dve.tensor_copy(bparts[0:1, 1, :], brest[0:1, :]))
                link(dve.tensor_tensor(brest[0:1, :], brest[0:1, :], bparts[0:1, 1, :], ALU.subtract))
                dve.tensor_copy(bparts[0:1, 2, :], brest[0:1, :]).then_inc(split_done, 1)
                dve.wait_ge(made, 4)
                dve.tensor_copy(trash[:, :], trash_i[:, :])
                dve.tensor_copy(earlier_b[:, :], earlier[:, :])

            @block.gpsimd
            def _(pool):
                pool.memset(ident[:, :], 0.0).then_inc(made, 1)
                pool.memset(earlier[:, :], 1.0).then_inc(made, 1)
                pool.wait_ge(made, 2)
                pool.affine_select(out=ident[:, :], in_=ident[:, :], compare_op=ALU.not_equal, fill=1.0, base=0,
                                   pattern=[[-1, P]], channel_multiplier=1)
                pool.affine_select(out=earlier[:, :], in_=earlier[:, :], compare_op=ALU.is_gt, fill=0.0, base=0,
                                   pattern=[[-1, P]], channel_multiplier=1).then_inc(made, 1)
                pool.iota(trash_i[:, :], pattern=[[P, WT]], base=TRASH, channel_multiplier=1).then_inc(made, 1)

            @block.sync
            def _(sp):
                sp.wait_ge(prepared, 1)
                for to, of in loads:
                    sp.dma_start(to, of).then_inc(loaded, 16)
                sp.wait_ge(split_done, 1)
                for r in range(3):
                    sp.dma_start(bias[r:r + 1, :], bparts[0:1, r, :]).then_inc(loaded, 16)
                sp.wait_ge(loaded, N_LOADS + 48)

        def edge_phase(n, table_in, table_out):
            c = ExitStack()
            with c:
                idx = [sb(f"idx{n}_{s}", [P, WT], I32, c) for s in range(2)]
                win = [sb(f"win{n}_{s}", [P, 2 * WT], F32, c) for s in range(2)]
                xg = [sb(f"xg{n}_{s}", [P, WT, D], F32, c) for s in range(2)]
                m = sb(f"m{n}", [P, WT, D], F32, c)
                part = [[sb(f"part{n}_{q}_{s}", [P, WT, D + 2], BF16, c) for q in range(3)] for s in range(2)]
                rows = [sb(f"rows{n}_{s}", [P, WE], F32, c) for s in range(2)]
                eq = [sb(f"eq{n}_{s}", [P, WT * (WE + P)], BF16, c) for s in range(2)]
                ms = [sb(f"ms{n}_{s}", [P, WT, D], F32, c) for s in range(2)]
                before = [sb(f"before{n}_{s}", [P, WT], F32, c) for s in range(2)]
                shift = [sb(f"shift{n}_{s}", [P, WT], F32, c) for s in range(2)]
                sidx = [sb(f"sidx{n}_{s}", [P, WT], I32, c) for s in range(2)]
                masked = sb(f"masked{n}", [P, WT, P], BF16, c)
                rowp = [pb(f"rowp{n}_{s}", c) for s in range(2)]
                sums = [pb(f"sums{n}_{s}", c) for s in range(2)]
                if n == 1:
                    nt_s = [sb(f"nt_s{s}", [P, 2, P], F32, c) for s in range(2)]
                    g1 = [sb(f"g1_{s}", [P, 2, P], F32, c) for s in range(2)]
                    g2 = [sb(f"g2_{s}", [P, WT, D], F32, c) for s in range(2)]
                    ffn = [pb(f"ffn{s}", c) for s in range(2)]
                    ffo = [pb(f"ffo{s}", c) for s in range(2)]

                idx_in = [sem(f"idx_in{n}_{s}") for s in range(2)]
                win_in = [sem(f"win_in{n}_{s}") for s in range(2)]
                gathered = [sem(f"gathered{n}_{s}") for s in range(2)]
                scattered = [sem(f"scattered{n}_{s}") for s in range(2)]
                rows_up = sem(f"rows_up{n}")
                rows_in = sem(f"rows_in{n}")
                compared = sem(f"compared{n}")
                counted = sem(f"counted{n}")
                messaged = sem(f"messaged{n}")
                summed = sem(f"summed{n}")
                copied = sem(f"copied{n}")
                indexed = sem(f"indexed{n}")
                shifted, masked_in, totalled, gated, multiplied, rest1, part0, part1 = (sem(f"{q}{n}") for q in (
                    "shifted", "masked_in", "totalled", "gated", "multiplied", "rest1_", "part0_", "part1_"))
                preset = sem(f"preset{n}")
                passed = sem(f"passed{n}")
                if n == 1:
                    turned = sem("turned")
                    turned_in = sem("turned_in")
                    mixed = sem("mixed")
                    gelu1 = sem("gelu1")
                    mixed2 = sem("mixed2")
                    gelu2 = sem("gelu2")

                with nc.Block() as block:
                    @block.sync
                    def _(sp):
                        def body(t, k):
                            s = k % 2
                            at, at4 = t.at(k, 1), t.at(k, WT)
                            t.wait_slot(gathered, k - 2, 16 * WT)
                            sp.dma_start(idx[s][:, :], gather_idx[n][:, bass.ds(at4, WT)]).then_inc(idx_in[s], 16)
                            t.wait(indexed, k - 2)
                            sp.dma_start(win[s][:, :], sw[n][:, bass.ds(at, 1), :].rearrange("p o b -> p (o b)")
                                         ).then_inc(win_in[s], 16)

                        def clear(table, done):
                            cleared = table.rearrange("(p r) f -> p (r f)", p=P)
                            for z in range(ZPARTS):
                                cut = slice(z * ZC // ZPARTS, (z + 1) * ZC // ZPARTS)
                                sp.dma_start(cleared[:, cut], zeros[:, :]).then_inc(done, 16)

                        for k in range(2):
                            body(Turns(sp, 2), k)
                            if n == 0 and k == 1:
                                for q in range(2):
                                    clear(agg[q], zeroed[q])
                        run_turns(sp, 2, 2, 2, NWIN // 2 - 1, NWIN - 1, body, (0, 1), ((1, 16 * WT),))
                        if n == 0:
                            sp.wait_ge(zeroed[1], 16 * ZPARTS)

                    @block.gpsimd
                    def _(pool):
                        def body(t, k):
                            s = k % 2
                            if k < NWIN or t.j is not None:
                                t.wait_slot(idx_in, k, 16)
                                t.wait(multiplied if n == 0 else turned, k - 2)
                                pool.sem_inc(passed, 1)
                                for b in range(WT):
                                    pool.indirect_dma_start(
                                        out=xg[s][:, b, :], out_offset=None, in_=table_in[:, :],
                                        in_offset=bass.IndirectOffsetOnAxis(ap=idx[s][:, b:b + 1], axis=0),
                                    ).then_inc(gathered[s], 16)
                            if k >= 2:
                                if k == 2 and n == 0 and t.j is None:
                                    pool.wait_ge(zeroed[0], 16 * ZPARTS)
                                t.wait(copied, k - 2)
                                t.wait(indexed, k - 2)
                                t.wait_slot(scattered, k - 3, 16 * WT)
                                pool.sem_inc(passed, 1)
                                for b in range(WT):
                                    pool.indirect_dma_start(
                                        out=table_out[:, :],
                                        out_offset=bass.IndirectOffsetOnAxis(ap=sidx[s][:, b:b + 1], axis=0),
                                        in_=ms[s][:, b, :], in_offset=None, compute_op=ALU.add,
                                    ).then_inc(scattered[s], 16)

                        run_turns(pool, 2, 0, 4, NWIN // 2 - 2, NWIN + 1, body, (2, 3),
                                  ((3, 16), (1, 16 * WT), (2, 16 * WT)))
                        for s in range(2):
                            pool.wait_ge(scattered[s], 16 * WT * (NWIN // 2))

                    @block.tensor
                    def _(pe):
                        def spread_rows(t, k):
                            t.wait_slot(win_in, k, 16)
                            t.wait(rows_in, k - 2)
                            for b in range(WT):
                                last = pe.transpose(rowp[k % 2][:, b * P:(b + 1) * P],
                                                    win[k % 2][:, b:b + 1].to_broadcast([P, P]), ident[:, :])
                            last.then_inc(rows_up, 1)

                        def transpose_neighbours(t, k):
                            s = k % 2
                            t.wait_slot(gathered, k, 16 * WT)
                            t.wait(gelu1, k - 2)
                            for q in range(2):
                                last = pe.transpose(ffn[s][:, q * P:(q + 1) * P],
                                                    xg[s][:, 2 * q:2 * q + 2, :].rearrange("p a f -> p (a f)"), ident[:, :])
                            last.then_inc(turned, 1)

                        def first_product(t, k):
                            s = k % 2
                            t.wait(turned_in, k)
                            pe.matmul(ffn[s][:, 256:512], wp1[:, :], nt_s[s][:, :, :].rearrange("p a f -> p (a f)"),
                                      start=True, stop=True).then_inc(mixed, 1)

                        def second_product(t, k):
                            s = k % 2
                            t.wait(gelu1, k)
                            t.wait(gelu2, k - 2)
                            pe.matmul(ffo[s][:, 0:WT * D], ones3[:, :], bias1, start=True, stop=False)
                            for q in range(2):
                                last = pe.matmul(ffo[s][:, q * P:(q + 1) * P], g1[s][:, q, :], wp2[:, :],
                                                 start=False, stop=(q == 1))
                            last.then_inc(mixed2, 1)

                        def add_equal(t, k):
                            s = k % 2
                            t.wait(compared, k)
                            t.wait(messaged, k)
                            t.wait(copied, k - 2)
                            t.wait(indexed, k - 2)
                            for a in range(WT):
                                for b in range(WT):
                                    same = eq[s][:, b * WE + a * P:b * WE + (a + 1) * P]
                                    for q in range(3):
                                        w = D + 1 if b < a and q == 0 else D
                                        last = pe.matmul(sums[s][:, a * (D + 1):a * (D + 1) + w], same,
                                                         part[s][q][:, b, 0:w], start=(b == q == 0),
                                                         stop=(b == WT - 1 and q == 2))
                            last.then_inc(summed, 1)

                        def body(t, k):
                            here, last = t.j is not None or k < NWIN, t.j is not None or k > 0
                            if here and n == 1:
                                transpose_neighbours(t, k)
                            if here:
                                spread_rows(t, k)
                            if here and n == 1:
                                first_product(t, k)
                            if last:
                                add_equal(t, k - 1)
                            if here and n == 1:
                                second_product(t, k)

                        run_turns(pe, 2, 0, 2, NWIN // 2 - 1, NWIN, body, range(-1, 4), ((2, 16), (2, 16 * WT)))

                    @block.scalar
                    def _(act):
                        if n == 1:
                            act.activation(g1[0][:, 0, 0:1], ident[:, 0:1], ACT.Gelu).then_inc(preset, 1)
                            act.wait_ge(preset, 1)

                        def rows_to_sbuf(t, k):
                            t.wait(rows_up, k)
                            t.wait(compared, k - 2)
                            act.activation(rows[k % 2][:, :], rowp[k % 2][:, :], ACT.Copy).then_inc(rows_in, 1)

                        def neighbours_to_sbuf(t, k):
                            s = k % 2
                            t.wait(turned, k)
                            act.activation(nt_s[s][:, :, :].rearrange("p a f -> p (a f)"), ffn[s][:, 0:256],
                                           ACT.Copy).then_inc(turned_in, 1)

                        def first_gelu(t, k):
                            s = k % 2
                            t.wait(mixed, k)
                            act.activation(g1[s][:, :, :].rearrange("p a f -> p (a f)"), ffn[s][:, 256:512],
                                           ACT.Gelu, bias=bp1[:, 0:1]).then_inc(gelu1, 1)

                        def second_gelu(t, k):
                            s = k % 2
                            t.wait(mixed2, k)
                            t.wait(multiplied, k - 2)
                            act.activation(g2[s][:, :, :].rearrange("p a f -> p (a f)"), ffo[s][:, 0:WT * D],
                                           ACT.Gelu).then_inc(gelu2, 1)

                        def sums_to_sbuf(t, k):
                            t.wait(totalled, k)
                            t.wait_slot(scattered, k - 2, 16 * WT)
                            act.activation(ms[k % 2][:, :, :],
                                           sums[k % 2][:, 0:WT * (D + 1)].rearrange("p (a f) -> p a f", a=WT)[:, :, 0:D],
                                           ACT.Copy).then_inc(copied, 1)

                        def body(t, k):
                            here, last = t.j is not None or k < NWIN, t.j is not None or k > 0
                            if here and n == 1:
                                neighbours_to_sbuf(t, k)
                            if here:
                                rows_to_sbuf(t, k)
                            if here and n == 1:
                                first_gelu(t, k)
                            if last:
                                sums_to_sbuf(t, k - 1)
                            if here and n == 1:
                                second_gelu(t, k)

                        run_turns(act, 2, 0, 2, NWIN // 2 - 1, NWIN, body, range(-1, 4), ((0, 16 * WT), (1, 16 * WT)))

                    @block.vector
                    def _(dve):
                        for s in range(2):
                            dve.memset(part[s][0][:, :, D:D + 2], 1.0)

                        def compare(t, k):
                            s = k % 2
                            t.wait(rows_in, k)
                            t.wait_slot(win_in, k, 16)
                            t.wait(summed, k - 2)
                            for b in range(WT):
                                last = dve.tensor_scalar(eq[s][:, b * WE:(b + 1) * WE], rows[s][:, :], win[s][:, b:b + 1], None,
                                                         ALU.is_equal)
                            last.then_inc(compared, 1)
                            t.wait(indexed, k - 2)
                            dve.tensor_tensor(shift[s][:, :], win[s][:, 0:WT], trash[:, :], ALU.subtract).then_inc(shifted, 1)
                            t.wait(compared, k)
                            t.wait(counted, k - 1)
                            own = eq[s][:, :].rearrange("p (b e) -> p b e", b=WT)[:, :, 0:P]
                            lower = earlier_b[:, :].rearrange("p (o e) -> p o e", o=1).to_broadcast([P, WT, P])
                            dve.tensor_tensor(masked[:, :, :], own, lower, ALU.mult).then_inc(masked_in, 1)
                            t.wait(masked_in, k)
                            dve.tensor_reduce(before[s][:, :], masked[:, :, :], AX_X, ALU.add).then_inc(counted, 1)

                        def message(t, k):
                            s = k % 2
                            if n == 0:
                                t.wait_slot(gathered, k, 16 * WT)
                                of = xg[s]
                            else:
                                t.wait(gelu2, k)
                                of = g2[s]
                            t.wait_slot(win_in, k, 16)
                            t.wait(messaged, k - 1)
                            wb = win[s][:, WT:2 * WT].rearrange("p (b o) -> p b o", o=1).to_broadcast([P, WT, D])
                            dve.tensor_tensor(m[:, :, :], of[:, :, :], wb, ALU.mult).then_inc(multiplied, 1)
                            cut = [part[s][q][:, :, 0:D] for q in range(3)]
                            t.wait(multiplied, k)
                            t.wait(summed, k - 2)
                            dve.tensor_copy(cut[0], m[:, :, :]).then_inc(part0, 1)
                            t.wait(part0, k)
                            dve.tensor_tensor(m[:, :, :], m[:, :, :], cut[0], ALU.subtract).then_inc(rest1, 1)
                            t.wait(rest1, k)
                            dve.tensor_copy(cut[1], m[:, :, :]).then_inc(part1, 1)
                            t.wait(part1, k)
                            dve.tensor_tensor(cut[2], m[:, :, :], cut[1], ALU.subtract).then_inc(messaged, 1)

                        def index(t, k):
                            s = k % 2
                            t.wait(summed, k)
                            t.wait(counted, k)
                            got = sums[s][:, 0:WT * (D + 1)].rearrange("p (a f) -> p a f", a=WT)[:, 1:WT, D]
                            dve.tensor_tensor(before[s][:, 1:WT], before[s][:, 1:WT], got, ALU.add).then_inc(totalled, 1)
                            t.wait(totalled, k)
                            t.wait(shifted, k)
                            dve.scalar_tensor_tensor(out=shift[s][:, :], in0=before[s][:, :], scalar=0.0, in1=shift[s][:, :],
                                                     op0=ALU.is_equal, op1=ALU.mult).then_inc(gated, 1)
                            t.wait(gated, k)
                            t.wait_slot(scattered, k - 2, 16 * WT)
                            dve.tensor_tensor(sidx[s][:, :], shift[s][:, :], trash[:, :], ALU.add).then_inc(indexed, 1)

                        def body(t, k):
                            here, last = t.j is not None or k < NWIN, t.j is not None or k > 0
                            if here and n == 0:
                                message(t, k)
                            if here:
                                compare(t, k)
                            if last:
                                index(t, k - 1)
                            if here and n == 1:
                                message(t, k)

                        run_turns(dve, 2, 0, 2, NWIN // 2 - 1, NWIN, body, range(-1, 4),
                                  ((0, 16 * WT), (1, 16 * WT), (2, 16 * WT), (2, 16)))

        def dense_phase(n):
            x_in, table_out = (x, x1) if n == 0 else (x1, out)
            c = ExitStack()
            with c:
                S = 4
                sums_of = agg[n][0:N, :]
                pair = [sb(f"pair{n}_{s}", [P, G, 2, D], F32, c) for s in range(S)]
                xs = [sb(f"xs{n}_{s}", [P, G, D], F32, c)[:, :, :] if n == 0 else pair[s][:, :, 0, :] for s in range(S)]
                y = [sb(f"y{n}_{s}", [P, G, D], F32, c) for s in range(S)]
                small = {q: [sb(f"{q}{n}_{s}", [P, G], F32, c) for s in range(S)]
                         for q in ("ssq", "inv", "mean", "var", "rstd")}
                mhalf = sb(f"mhalf{n}", [P, G], F32, c)
                sq_a, sq_b = (sb(f"sq_{q}{n}", [P, G, D], F32, c) for q in "ab")
                turned_s = [sb(f"turned_s{n}_{h}", [P, GH * P], F32, c) for h in range(2)]
                turned_p = [pb(f"turned_p{n}_{h}", c) for h in range(2)]
                if n == 0:
                    relu = [sb(f"relu_{h}", [P, GH, 2 * D], F32, c) for h in range(2)]
                    zp = [c.enter_context(nc.psum_tensor(f"zp{h}", [P, GH, 256], F32)) for h in range(2)]
                else:
                    hid_s = [sb(f"hid_s{s}", [P, GH * P], F32, c) for s in range(2)]
                    hid_p = [pb(f"hid_p{s}", c) for s in range(2)]
                    out_p = [pb(f"out_p{s}", c) for s in range(2)]

                loads = [sem(f"loads{n}_{s}") for s in range(S)]
                stores = [sem(f"stores{n}_{s}") for s in range(S)]
                mhalf_in = sem(f"mhalf_in{n}")
                passed = sem(f"passed_d{n}")
                two = lambda name: [sem(f"{name}{n}_{h}") for h in range(2)]
                turned = two("turned_d")
                turned_in = two("turned_in_d")
                (squared, ssq_in, ssq_ready, inv_ready, scaled, added, mean_in, centred, squared2, var_in, var_ready,
                 rstd_ready, normed) = (sem(f"{q}{n}") for q in (
                     "squared", "ssq_in", "ssq_ready", "inv_ready", "scaled", "added", "mean_in", "centred", "squared2",
                     "var_in", "var_ready", "rstd_ready", "normed"))
                if n == 0:
                    product = sem("product")
                    z_up, relu_in, half_added, y_half = two("z_up"), two("relu_in"), two("half_added"), two("y_half")
                    y_made = y_half[1]
                    LAG = 0
                else:
                    hid_up = two("hid_up")
                    hid_in = sem("hid_in")
                    out_up = sem("out_up")
                    y_made = sem("y_made")
                    LAG = 1
                START = 4
                TURNS = (NCH - START - 2) // 4

                def wide(t):
                    return t[:, :].rearrange("p (g o) -> p g o", o=1).to_broadcast([P, G, D])

                def flat(t):
                    return t.rearrange("p g f -> p (g f)")

                with nc.Block() as block:
                    @block.sync
                    def _(sp):
                        def rows_of(table, t, k):
                            at = t.at(k, CR)
                            if t.j is None and k == NCH - 1:
                                return table[at:at + TAIL, :].rearrange("(p g) f -> p g f", g=TG), TP, TG
                            return table[bass.ds(at, CR), :].rearrange("(p g) f -> p g f", g=G), P, G

                        def body(t, k):
                            load, store = k + 3, k - 2 - LAG
                            if t.j is not None or load < NCH:
                                s = load % S
                                xr, p, g = rows_of(x_in, t, load)
                                ar, p, g = rows_of(sums_of, t, load)
                                t.wait(added, load - 4)
                                t.wait(turned[1], load - 4)
                                sp.dma_start(xs[s][0:p, 0:g, :], xr).then_inc(loads[s], 16)
                                sp.dma_start(pair[s][0:p, 0:g, 1, :], ar).then_inc(loads[s], 16)
                            if t.j is not None or 0 <= store < NCH:
                                s = store % S
                                to, p, g = rows_of(table_out, t, store)
                                t.wait(normed, store)
                                sp.dma_start(to, y[s][0:p, 0:g, :]).then_inc(stores[s], 16)

                        run_turns(sp, 4, -3, START, TURNS - 1, NCH + 1 + LAG, body, range(START - 3, START + 3))
                        for s in range(S):
                            sp.wait_ge(stores[s], 16 * len(range(s, NCH, S)))

                    @block.gpsimd
                    def _(pool):
                        pool.memset(mhalf[:, :], -0.5).then_inc(mhalf_in, 1)
                        pool.wait_ge(mhalf_in, 1)

                        def body(t, k):
                            live = lambda q: t.j is not None or 0 <= q < NCH
                            q = k - 1 - LAG
                            if live(q):
                                s = q % S
                                t.wait(scaled, q)
                                pool.tensor_tensor(y[s][:, :, :], y[s][:, :, :], xs[s], ALU.add).then_inc(added, 1)
                            q = k + 2
                            if n == 0 and live(q):
                                s = q % S
                                t.wait_slot(loads, q, 32)
                                t.wait(turned[1], q - 4)
                                pool.tensor_tensor(pair[s][:, :, 0, :], xs[s], pair[s][:, :, 1, :], ALU.mult
                                                   ).then_inc(product, 1)
                            q = k - 2 - LAG
                            if live(q):
                                s = q % S
                                t.wait(var_ready, q)
                                pool.tensor_tensor(small["rstd"][s][:, :], small["var"][s][:, :], mhalf[:, :], ALU.pow
                                                   ).then_inc(rstd_ready, 1)
                            q = k - LAG
                            if live(q):
                                s = q % S
                                t.wait(ssq_ready, q)
                                pool.tensor_tensor(small["inv"][s][:, :], small["ssq"][s][:, :], mhalf[:, :], ALU.pow
                                                   ).then_inc(inv_ready, 1)

                        run_turns(pool, 4, -2, START, TURNS, NCH + 1 + LAG, body, range(START - 3, START + 4),
                                  ((2, 32), (3, 32)) if n == 0 else ())

                    @block.tensor
                    def _(pe):
                        def transpose_pair(t, k):
                            s = k % S
                            if n == 0:
                                t.wait(product, k)
                            else:
                                t.wait_slot(loads, k, 32)
                            for h in range(2):
                                t.wait(turned_in[h], k - 1)
                                for g in range(GH):
                                    last = pe.transpose(turned_p[h][:, g * P:(g + 1) * P], pair[s][:, h * GH + g, :, :].rearrange("p a f -> p (a f)"),
                                                        ident[:, :])
                                last.then_inc(turned[h], 1)

                        def products(t, k):
                            for h in range(2):
                                t.wait(turned_in[h], k)
                                t.wait(half_added[h], k - 1)
                                for g in range(0, GH, 2):
                                    pe.matmul(zp[h][:, g:g + 2, 0:3 * D], ones3[:, :],
                                              bias0.rearrange("p (g f) -> p g f", g=2), start=True, stop=False)
                                    for e in range(2):
                                        last = pe.matmul(zp[h][:, g + e, 0:3 * D],
                                                         turned_s[h][:, (g + e) * P:(g + e + 1) * P], wz[:, :],
                                                         start=False, stop=(e == 1))
                                last.then_inc(z_up[h], 1)

                        def hidden(t, k):
                            for h in range(2):
                                t.wait(turned_in[h], k)
                                t.wait(hid_in, k - 2)
                                pe.matmul(hid_p[k % 2][h * D:(h + 1) * D, :], wu1[:, :], turned_s[h][:, :],
                                          start=True, stop=True).then_inc(hid_up[h], 1)

                        def outputs(t, k):
                            t.wait(hid_in, k)
                            t.wait(y_made, k - 2)
                            pe.matmul(out_p[k % 2][:, :], ones3[:, :], bias2, start=True, stop=False)
                            to = out_p[k % 2][:, :].rearrange("p (h g f) -> p h g f", h=2, g=GH)
                            for g in range(GH):
                                last = pe.matmul(to[:, :, g, :], hid_s[k % 2][:, g * P:(g + 1) * P], wu2[:, :],
                                                 start=False, stop=(g == GH - 1))
                            last.then_inc(out_up, 1)

                        def body(t, k):
                            live = lambda q: t.j is not None or 0 <= q < NCH
                            if n == 0:
                                if live(k + 1):
                                    transpose_pair(t, k + 1)
                                if live(k):
                                    products(t, k)
                            else:
                                if live(k):
                                    hidden(t, k)
                                if live(k - 1):
                                    outputs(t, k - 1)
                                if live(k + 1):
                                    transpose_pair(t, k + 1)

                        run_turns(pe, 4, -1, START, TURNS, NCH, body, range(START - 3, START + 5), ((2, 32), (3, 32)))

                    @block.scalar
                    def _(act):
                        if n == 1:
                            act.activation(hid_s[0][:, 0:1], ident[:, 0:1], ACT.Gelu).then_inc(passed, 1)
                            act.wait_ge(passed, 1)

                        def turned_to_sbuf(t, k):
                            for h in range(2):
                                t.wait(turned[h], k)
                                t.wait(z_up[h] if n == 0 else hid_up[h], k - 1)
                                act.activation(turned_s[h][:, :], turned_p[h][:, :], ACT.Copy).then_inc(turned_in[h], 1)

                        def relus(t, k):
                            for h in range(2):
                                t.wait(z_up[h], k)
                                t.wait(y_half[h], k - 1)
                                act.activation(relu[h][:, :, :], zp[h][:, :, 0:2 * D], ACT.Relu, scale=1.0 - SLOPE
                                               ).then_inc(relu_in[h], 1)

                        def gelu_hidden(t, k):
                            t.wait(hid_up[1], k)
                            t.wait(out_up, k - 2)
                            act.activation(hid_s[k % 2][:, :], hid_p[k % 2][:, :], ACT.Gelu, bias=bu1[:, 0:1]
                                           ).then_inc(hid_in, 1)

                        def gelu_out(t, k):
                            t.wait(out_up, k)
                            t.wait_slot(stores, k - 4, 16)
                            act.activation(flat(y[k % S][:, :, :]), out_p[k % 2][:, :], ACT.Gelu).then_inc(y_made, 1)

                        def square(t, k):
                            t.wait(y_made, k)
                            t.wait(ssq_in, k - 1)
                            act.activation(sq_a[:, :, :], y[k % S][:, :, :], ACT.Square).then_inc(squared, 1)

                        def square_centred(t, k):
                            t.wait(centred, k)
                            t.wait(var_in, k - 1)
                            act.activation(sq_b[:, :, :], y[k % S][:, :, :], ACT.Square, scale=D ** -0.5
                                           ).then_inc(squared2, 1)

                        def body(t, k):
                            live = lambda q: t.j is not None or 0 <= q < NCH
                            if n == 0 and live(k):
                                relus(t, k)
                            if n == 1 and live(k):
                                gelu_hidden(t, k)
                            if n == 1 and live(k - 1):
                                gelu_out(t, k - 1)
                                square(t, k - 1)
                            if live(k + 1):
                                turned_to_sbuf(t, k + 1)
                            if n == 0 and live(k):
                                square(t, k)
                            if live(k - 1 - LAG):
                                square_centred(t, k - 1 - LAG)

                        run_turns(act, 4, -1, START, TURNS, NCH + LAG, body, range(START - 3, START + 5),
                                  ((0, 16), (1, 16)))

                    @block.vector
                    def _(dve):
                        def leaky(t, k):
                            s = k % S
                            for h in range(2):
                                half = slice(h * GH, (h + 1) * GH)
                                t.wait(relu_in[h], k)
                                t.wait_slot(stores, k - 4, 16)
                                dve.tensor_tensor(y[s][:, half, :], relu[h][:, :, 0:D], zp[h][:, :, 2 * D:3 * D], ALU.add
                                                  ).then_inc(half_added[h], 1)
                            for h in range(2):
                                half = slice(h * GH, (h + 1) * GH)
                                t.wait(half_added[h], k)
                                dve.tensor_tensor(y[s][:, half, :], y[s][:, half, :], relu[h][:, :, D:2 * D], ALU.add
                                                  ).then_inc(y_half[h], 1)

                        def sum_squares(t, k):
                            ssq = small["ssq"][k % S]
                            t.wait(squared, k)
                            dve.tensor_reduce(ssq[:, :], sq_a[:, :, :], AX_X, ALU.add).then_inc(ssq_in, 1)
                            t.wait(ssq_in, k)
                            dve.tensor_scalar(ssq[:, :], ssq[:, :], L2_EPS, None, ALU.max).then_inc(ssq_ready, 1)

                        def scale(t, k):
                            s = k % S
                            t.wait(inv_ready, k)
                            dve.tensor_tensor(y[s][:, :, :], y[s][:, :, :], wide(small["inv"][s]), ALU.mult
                                              ).then_inc(scaled, 1)

                        def centre(t, k):
                            s = k % S
                            t.wait(added, k)
                            dve.tensor_reduce(small["mean"][s][:, :], y[s][:, :, :], AX_X, ALU.add).then_inc(mean_in, 1)
                            t.wait(mean_in, k)
                            dve.scalar_tensor_tensor(out=y[s][:, :, :], in0=wide(small["mean"][s]), scalar=-1.0 / D,
                                                     in1=y[s][:, :, :], op0=ALU.mult, op1=ALU.add).then_inc(centred, 1)

                        def variance(t, k):
                            var = small["var"][k % S]
                            t.wait(squared2, k)
                            dve.tensor_reduce(var[:, :], sq_b[:, :, :], AX_X, ALU.add).then_inc(var_in, 1)
                            t.wait(var_in, k)
                            dve.tensor_scalar(var[:, :], var[:, :], LN_EPS, None, ALU.add).then_inc(var_ready, 1)

                        def normalize(t, k):
                            s = k % S
                            t.wait(rstd_ready, k)
                            dve.tensor_tensor(y[s][:, :, :], y[s][:, :, :], wide(small["rstd"][s]), ALU.mult
                                              ).then_inc(normed, 1)

                        if n == 1:
                            pass

                        def body(t, k):
                            live = lambda q: t.j is not None or 0 <= q < NCH
                            if live(k - 1 - LAG):
                                scale(t, k - 1 - LAG)
                            if n == 0 and live(k):
                                leaky(t, k)
                            if live(k - 2 - LAG):
                                variance(t, k - 2 - LAG)
                            if live(k - LAG):
                                sum_squares(t, k - LAG)
                            if live(k - 1 - LAG):
                                centre(t, k - 1 - LAG)
                            if live(k - 2 - LAG):
                                normalize(t, k - 2 - LAG)

                        run_turns(dve, 4, 0, START, TURNS, NCH + 1 + LAG, body, range(START - 3, START + 4),
                                  ((0, 16), (1, 16)))

        edge_phase(0, x, agg[0])
        dense_phase(0)
        edge_phase(1, x1, agg[1])
        dense_phase(1)


_INS = ['x', 'src', 'dst', 'edge_weight', 'L0_gnn_W1', 'L0_gnn_W2', 'L0_gnn_b1', 'L0_gnn_b2', 'L1_gnn_W1p', 'L1_gnn_b1p',
        'L1_gnn_W2p', 'L1_gnn_b2p', 'L1_gnn_W1u', 'L1_gnn_b1u', 'L1_gnn_W2u', 'L1_gnn_b2u']


def kernel(**inputs):
    import numpy as _np
    import concourse.bacc as _bacc
    from concourse import mybir as _mybir
    from concourse.bass_utils import run_bass_kernel_spmd as _run

    nc = _bacc.Bacc("TRN2", target_bir_lowering=False, num_devices=1)
    arrays, args = {}, []
    for name in _INS:
        a = _np.ascontiguousarray(inputs[name])
        arrays[f"in_{name}"] = a
        args.append(nc.dram_tensor(f"in_{name}", a.shape, _mybir.dt.from_np(a.dtype), kind="ExternalInput").ap())
    args.append(nc.dram_tensor("out_0", arrays["in_x"].shape, _mybir.dt.float32, kind="ExternalOutput").ap())
    gnn_kernel(nc, *args)
    r = _run(nc, [arrays], core_ids=[0])
    return r.results[0]["out_0"]
```

```python
import numpy as np
import concourse.bass as bass
from concourse import mybir
from contextlib import ExitStack

F32 = mybir.dt.float32
BF16 = mybir.dt.bfloat16
I32 = mybir.dt.int32
ALU = mybir.AluOpType
ACT = mybir.ActivationFunctionType
AX_X = mybir.AxisListType.X

P = 128
D = 64
WT = 4
WE = WT * P
G = 8
CR = P * G
FW = G * D
GH = G // 2
L2_EPS = 1e-12
LN_EPS = 1e-5
SLOPE = 0.2


class Turns:

    def __init__(self, eng, per, j=None, counts=(), laps=()):
        self.eng, self.per, self.j = eng, per, j
        if j is not None:
            self.count = {k: eng.snap(j * per + (k + 1)) for k in counts}
            self.lap = {(n, times): eng.snap(j * times + n * times) for n, times in laps}

    def wait(self, sem, k):
        if self.j is not None:
            self.eng.wait_ge(sem, self.count[k])
        elif k >= 0:
            self.eng.wait_ge(sem, k + 1)

    def wait_slot(self, sems, k, times):
        n = k // self.per + 1
        if self.j is not None:
            self.eng.wait_ge(sems[k % self.per], self.lap[n, times])
        elif n > 0:
            self.eng.wait_ge(sems[k % self.per], n * times)

    def at(self, k, size):
        return k * size if self.j is None else self.eng.snap(self.j * (self.per * size) + k * size)


def run_turns(eng, per, first, start, turns, last, body, counts=(), laps=()):
    for k in range(first, start):
        body(Turns(eng, per), k)
    with eng.Fori(0, turns) as j:
        t = Turns(eng, per, j, counts, laps)
        for k in range(start, start + per):
            body(t, k)
    for k in range(start + turns * per, last + 1):
        body(Turns(eng, per), k)


def gnn_kernel(nc, x, src, dst, edge_weight, w1a, w2a, b1a, b2a, w1p, b1p, w2p, b2p, w1u, b1u, w2u, b2u, out):
    N = x.shape[0]
    E = src.shape[0]
    EC = E // P
    ER = E - EC * P
    NWIN = 2 * -(-E // (2 * WE))
    TILES = NWIN * WT
    assert TILES > EC
    NCH = -(-N // CR)
    TAIL = N - (NCH - 1) * CR
    TG = next(g for g in range(G, 0, -1) if TAIL % g == 0 and TAIL // g <= P)
    TP = TAIL // TG
    TRASH = N + 1
    AROWS = P * -(-(TRASH + WE) // P)
    ZC = AROWS // P * D
    ZPARTS = next(z for z in range(6, 100) if ZC % z == 0)

    x1 = nc.dram_tensor("x1", (N, D), F32, kind="Internal").ap()
    agg = [nc.dram_tensor(f"agg{n}", (AROWS, D), F32, kind="Internal").ap() for n in range(2)]

    ctx = ExitStack()
    with ctx:
        def sb(name, shape, dt=F32, c=ctx):
            return c.enter_context(nc.sbuf_tensor(name, shape, dt))

        def pb(name, c):
            return c.enter_context(nc.psum_tensor(name, [P, 512], F32))

        def sem(name, c=ctx):
            return c.enter_context(nc.semaphore(name))

        gather_idx = [sb(f"gather_idx{n}", [P, TILES], I32) for n in range(2)]
        scatter_raw = [sb(f"scatter_raw{n}", [P, TILES], I32) for n in range(2)]
        ew = sb("ew", [P, TILES])
        sw = [sb(f"sw{n}", [P, NWIN, 2 * WT]) for n in range(2)]
        ident = sb("ident", [P, P])
        earlier = sb("earlier", [P, P])
        earlier_b = sb("earlier_b", [P, P], BF16)
        trash_i = sb("trash_i", [P, WT], I32)
        trash = sb("trash", [P, WT])
        ones3 = sb("ones3", [P, P], BF16)
        wz = sb("wz", [P, 3 * D])
        wp1 = sb("wp1", [P, P])
        wp2 = sb("wp2", [P, P])
        wu1 = sb("wu1", [P, D])
        wu2 = sb("wu2", [P, P])
        bp1 = sb("bp1", [P, 1])
        bu1 = sb("bu1", [P, 1])
        NB0, NB1, NB2 = 2 * 3 * D, WT * D, G * D
        NB = NB0 + NB1 + NB2
        brow = sb("brow", [1, NB])
        brest = sb("brest", [1, NB])
        bparts = sb("bparts", [1, 3, NB], BF16)
        bias = sb("bias", [P, NB], BF16)
        bias0, bias1, bias2 = bias[:, 0:NB0], bias[:, NB0:NB0 + NB1], bias[:, NB0 + NB1:NB]
        zeros = sb("zeros", [P, ZC // ZPARTS])

        loaded = sem("loaded")
        prepared = sem("prepared")
        made = sem("made")
        chain = sem("chain")
        split_done = sem("split_done")
        zeroed = [sem(f"zeroed{n}") for n in range(2)]

        with nc.Block() as block:
            loads = []
            for t, pad, s in ((gather_idx[0], 0, src), (gather_idx[1], 0, dst),
                              (scatter_raw[0], N, dst), (scatter_raw[1], N, src), (ew, 0, edge_weight)):
                loads.append((t[:, 0:EC], s[0:EC * P].rearrange("(p t) -> p t", p=P)))
                if ER:
                    loads.append((t[0:ER, EC:EC + 1], s[EC * P:E].rearrange("(p t) -> p t", t=1)))
            for t, w in ((wp1, w1p), (wp2, w2p), (wu2, w2u)):
                loads += [(t[0:D, 0:D], w), (t[D:2 * D, D:2 * D], w)]
            loads += [(wz[0:D, 0:D], w1a), (wz[D:2 * D, D:2 * D], w2a),
                      (wz[0:D, 2 * D:3 * D], w1a), (wz[D:2 * D, 2 * D:3 * D], w2a), (wu1[:, :], w1u)]
            for t, b in ((bp1, b1p), (bu1, b1u)):
                for h in range(2):
                    loads.append((t[h * D:(h + 1) * D, 0:1], b.rearrange("(f o) -> f o", o=1)))
            for h in range(2):
                loads += [(brow[0:1, (3 * h) * D:(3 * h + 1) * D], b1a), (brow[0:1, (3 * h + 1) * D:(3 * h + 2) * D], b2a)]
            for g in range(WT):
                loads.append((brow[0:1, NB0 + g * D:NB0 + (g + 1) * D], b2p.rearrange("(o f) -> o f", o=1)))
            for g in range(G):
                loads.append((brow[0:1, NB0 + NB1 + g * D:NB0 + NB1 + (g + 1) * D], b2u.rearrange("(o f) -> o f", o=1)))
            N_LOADS = 16 * len(loads)

            @block.vector
            def _(dve):
                for t, pad in ((gather_idx[0], 0), (gather_idx[1], 0), (scatter_raw[0], N), (scatter_raw[1], N)):
                    dve.memset(t[:, EC:TILES], pad)
                dve.memset(ew[:, EC:TILES], 0.0)
                for t in (wp1, wp2, wu2, wz):
                    dve.memset(t[:, :], 0.0)
                dve.memset(bias[:, :], 0.0)
                dve.memset(ones3[:, :], 0.0).then_inc(prepared, 1)
                dve.memset(zeros[:, :], 0.0).then_inc(prepared, 1)
                dve.wait_ge(prepared, 2)
                dve.memset(ones3[0:3, :], 1.0)
                dve.wait_ge(loaded, N_LOADS)
                for n in range(2):
                    dve.tensor_copy(sw[n][:, :, 0:WT], scatter_raw[n][:, :].rearrange("p (k b) -> p k b", b=WT))
                    dve.tensor_copy(sw[n][:, :, WT:2 * WT], ew[:, :].rearrange("p (k b) -> p k b", b=WT))
                dve.tensor_scalar(wz[:, 2 * D:3 * D], wz[:, 2 * D:3 * D], SLOPE, None, ALU.mult)
                b0 = brow[0:1, 0:NB0].rearrange("o (h k f) -> o h k f", h=2, k=3)
                step = 0

                def link(ins):
                    nonlocal step
                    step += 1
                    ins.then_inc(chain, 1)
                    dve.wait_ge(chain, step)

                link(dve.tensor_tensor(b0[:, :, 2, :], b0[:, :, 0, :], b0[:, :, 1, :], ALU.add))
                link(dve.tensor_scalar(b0[:, :, 2, :], b0[:, :, 2, :], SLOPE, None, ALU.mult))
                link(dve.tensor_copy(bparts[0:1, 0, :], brow[0:1, :]))
                link(dve.tensor_tensor(brest[0:1, :], brow[0:1, :], bparts[0:1, 0, :], ALU.subtract))
                link(dve.tensor_copy(bparts[0:1, 1, :], brest[0:1, :]))
                link(dve.tensor_tensor(brest[0:1, :], brest[0:1, :], bparts[0:1, 1, :], ALU.subtract))
                dve.tensor_copy(bparts[0:1, 2, :], brest[0:1, :]).then_inc(split_done, 1)
                dve.wait_ge(made, 4)
                dve.tensor_copy(trash[:, :], trash_i[:, :])
                dve.tensor_copy(earlier_b[:, :], earlier[:, :])

            @block.gpsimd
            def _(pool):
                pool.memset(ident[:, :], 0.0).then_inc(made, 1)
                pool.memset(earlier[:, :], 1.0).then_inc(made, 1)
                pool.wait_ge(made, 2)
                pool.affine_select(out=ident[:, :], in_=ident[:, :], compare_op=ALU.not_equal, fill=1.0, base=0,
                                   pattern=[[-1, P]], channel_multiplier=1)
                pool.affine_select(out=earlier[:, :], in_=earlier[:, :], compare_op=ALU.is_gt, fill=0.0, base=0,
                                   pattern=[[-1, P]], channel_multiplier=1).then_inc(made, 1)
                pool.iota(trash_i[:, :], pattern=[[P, WT]], base=TRASH, channel_multiplier=1).then_inc(made, 1)

            @block.sync
            def _(sp):
                sp.wait_ge(prepared, 1)
                for to, of in loads:
                    sp.dma_start(to, of).then_inc(loaded, 16)
                sp.wait_ge(split_done, 1)
                for r in range(3):
                    sp.dma_start(bias[r:r + 1, :], bparts[0:1, r, :]).then_inc(loaded, 16)
                sp.wait_ge(loaded, N_LOADS + 48)

        def edge_phase(n, table_in, table_out):
            c = ExitStack()
            with c:
                idx = [sb(f"idx{n}_{s}", [P, WT], I32, c) for s in range(2)]
                win = [sb(f"win{n}_{s}", [P, 2 * WT], F32, c) for s in range(2)]
                xg = [sb(f"xg{n}_{s}", [P, WT, D], F32, c) for s in range(2)]
                m = sb(f"m{n}", [P, WT, D], F32, c)
                part = [[sb(f"part{n}_{q}_{s}", [P, WT, D + 2], BF16, c) for q in range(3)] for s in range(2)]
                rows = [sb(f"rows{n}_{s}", [P, WE], F32, c) for s in range(2)]
                eq = [sb(f"eq{n}_{s}", [P, WT * (WE + P)], BF16, c) for s in range(2)]
                ms = [sb(f"ms{n}_{s}", [P, WT, D], F32, c) for s in range(2)]
                before = [sb(f"before{n}_{s}", [P, WT], F32, c) for s in range(2)]
                shift = [sb(f"shift{n}_{s}", [P, WT], F32, c) for s in range(2)]
                sidx = [sb(f"sidx{n}_{s}", [P, WT], I32, c) for s in range(2)]
                masked = sb(f"masked{n}", [P, WT, P], BF16, c)
                rowp = [pb(f"rowp{n}_{s}", c) for s in range(2)]
                sums = [pb(f"sums{n}_{s}", c) for s in range(2)]
                if n == 1:
                    nt_s = [sb(f"nt_s{s}", [P, 2, P], F32, c) for s in range(2)]
                    g1 = [sb(f"g1_{s}", [P, 2, P], F32, c) for s in range(2)]
                    g2 = [sb(f"g2_{s}", [P, WT, D], F32, c) for s in range(2)]
                    ffn = [pb(f"ffn{s}", c) for s in range(2)]
                    ffo = [pb(f"ffo{s}", c) for s in range(2)]

                idx_in = [sem(f"idx_in{n}_{s}") for s in range(2)]
                win_in = [sem(f"win_in{n}_{s}") for s in range(2)]
                gathered = [sem(f"gathered{n}_{s}") for s in range(2)]
                scattered = [sem(f"scattered{n}_{s}") for s in range(2)]
                rows_up = sem(f"rows_up{n}")
                rows_in = sem(f"rows_in{n}")
                compared = sem(f"compared{n}")
                counted = sem(f"counted{n}")
                messaged = sem(f"messaged{n}")
                summed = sem(f"summed{n}")
                copied = sem(f"copied{n}")
                indexed = sem(f"indexed{n}")
                shifted, masked_in, totalled, gated, multiplied, rest1, part0, part1 = (sem(f"{q}{n}") for q in (
                    "shifted", "masked_in", "totalled", "gated", "multiplied", "rest1_", "part0_", "part1_"))
                preset = sem(f"preset{n}")
                passed = sem(f"passed{n}")
                if n == 1:
                    turned = sem("turned")
                    turned_in = sem("turned_in")
                    mixed = sem("mixed")
                    gelu1 = sem("gelu1")
                    mixed2 = sem("mixed2")
                    gelu2 = sem("gelu2")

                with nc.Block() as block:
                    @block.sync
                    def _(sp):
                        def body(t, k):
                            s = k % 2
                            at, at4 = t.at(k, 1), t.at(k, WT)
                            t.wait_slot(gathered, k - 2, 16 * WT)
                            sp.dma_start(idx[s][:, :], gather_idx[n][:, bass.ds(at4, WT)]).then_inc(idx_in[s], 16)
                            t.wait(indexed, k - 2)
                            sp.dma_start(win[s][:, :], sw[n][:, bass.ds(at, 1), :].rearrange("p o b -> p (o b)")
                                         ).then_inc(win_in[s], 16)

                        def clear(table, done):
                            cleared = table.rearrange("(p r) f -> p (r f)", p=P)
                            for z in range(ZPARTS):
                                cut = slice(z * ZC // ZPARTS, (z + 1) * ZC // ZPARTS)
                                sp.dma_start(cleared[:, cut], zeros[:, :]).then_inc(done, 16)

                        for k in range(2):
                            body(Turns(sp, 2), k)
                            if n == 0 and k == 1:
                                for q in range(2):
                                    clear(agg[q], zeroed[q])
                        run_turns(sp, 2, 2, 2, NWIN // 2 - 1, NWIN - 1, body, (0, 1), ((1, 16 * WT),))
                        if n == 0:
                            sp.wait_ge(zeroed[1], 16 * ZPARTS)

                    @block.gpsimd
                    def _(pool):
                        def body(t, k):
                            s = k % 2
                            if k < NWIN or t.j is not None:
                                t.wait_slot(idx_in, k, 16)
                                t.wait(multiplied if n == 0 else turned, k - 2)
                                pool.sem_inc(passed, 1)
                                for b in range(WT):
                                    pool.indirect_dma_start(
                                        out=xg[s][:, b, :], out_offset=None, in_=table_in[:, :],
                                        in_offset=bass.IndirectOffsetOnAxis(ap=idx[s][:, b:b + 1], axis=0),
                                    ).then_inc(gathered[s], 16)
                            if k >= 2:
                                if k == 2 and n == 0 and t.j is None:
                                    pool.wait_ge(zeroed[0], 16 * ZPARTS)
                                t.wait(copied, k - 2)
                                t.wait(indexed, k - 2)
                                t.wait_slot(scattered, k - 3, 16 * WT)
                                pool.sem_inc(passed, 1)
                                for b in range(WT):
                                    pool.indirect_dma_start(
                                        out=table_out[:, :],
                                        out_offset=bass.IndirectOffsetOnAxis(ap=sidx[s][:, b:b + 1], axis=0),
                                        in_=ms[s][:, b, :], in_offset=None, compute_op=ALU.add,
                                    ).then_inc(scattered[s], 16)

                        run_turns(pool, 2, 0, 4, NWIN // 2 - 2, NWIN + 1, body, (2, 3),
                                  ((3, 16), (1, 16 * WT), (2, 16 * WT)))
                        for s in range(2):
                            pool.wait_ge(scattered[s], 16 * WT * (NWIN // 2))

                    @block.tensor
                    def _(pe):
                        def spread_rows(t, k):
                            t.wait_slot(win_in, k, 16)
                            t.wait(rows_in, k - 2)
                            for b in range(WT):
                                last = pe.transpose(rowp[k % 2][:, b * P:(b + 1) * P],
                                                    win[k % 2][:, b:b + 1].to_broadcast([P, P]), ident[:, :])
                            last.then_inc(rows_up, 1)

                        def transpose_neighbours(t, k):
                            s = k % 2
                            t.wait_slot(gathered, k, 16 * WT)
                            t.wait(gelu1, k - 2)
                            for q in range(2):
                                last = pe.transpose(ffn[s][:, q * P:(q + 1) * P],
                                                    xg[s][:, 2 * q:2 * q + 2, :].rearrange("p a f -> p (a f)"), ident[:, :])
                            last.then_inc(turned, 1)

                        def first_product(t, k):
                            s = k % 2
                            t.wait(turned_in, k)
                            pe.matmul(ffn[s][:, 256:512], wp1[:, :], nt_s[s][:, :, :].rearrange("p a f -> p (a f)"),
                                      start=True, stop=True).then_inc(mixed, 1)

                        def second_product(t, k):
                            s = k % 2
                            t.wait(gelu1, k)
                            t.wait(gelu2, k - 2)
                            pe.matmul(ffo[s][:, 0:WT * D], ones3[:, :], bias1, start=True, stop=False)
                            for q in range(2):
                                last = pe.matmul(ffo[s][:, q * P:(q + 1) * P], g1[s][:, q, :], wp2[:, :],
                                                 start=False, stop=(q == 1))
                            last.then_inc(mixed2, 1)

                        def add_equal(t, k):
                            s = k % 2
                            t.wait(compared, k)
                            t.wait(messaged, k)
                            t.wait(copied, k - 2)
                            t.wait(indexed, k - 2)
                            for a in range(WT):
                                for b in range(WT):
                                    same = eq[s][:, b * WE + a * P:b * WE + (a + 1) * P]
                                    for q in range(3):
                                        w = D + 1 if b < a and q == 0 else D
                                        last = pe.matmul(sums[s][:, a * (D + 1):a * (D + 1) + w], same,
                                                         part[s][q][:, b, 0:w], start=(b == q == 0),
                                                         stop=(b == WT - 1 and q == 2))
                            last.then_inc(summed, 1)

                        def body(t, k):
                            here, last = t.j is not None or k < NWIN, t.j is not None or k > 0
                            if here and n == 1:
                                transpose_neighbours(t, k)
                            if here:
                                spread_rows(t, k)
                            if here and n == 1:
                                first_product(t, k)
                            if last:
                                add_equal(t, k - 1)
                            if here and n == 1:
                                second_product(t, k)

                        run_turns(pe, 2, 0, 2, NWIN // 2 - 1, NWIN, body, range(-1, 4), ((2, 16), (2, 16 * WT)))

                    @block.scalar
                    def _(act):
                        if n == 1:
                            act.activation(g1[0][:, 0, 0:1], ident[:, 0:1], ACT.Gelu).then_inc(preset, 1)
                            act.wait_ge(preset, 1)

                        def rows_to_sbuf(t, k):
                            t.wait(rows_up, k)
                            t.wait(compared, k - 2)
                            act.activation(rows[k % 2][:, :], rowp[k % 2][:, :], ACT.Copy).then_inc(rows_in, 1)

                        def neighbours_to_sbuf(t, k):
                            s = k % 2
                            t.wait(turned, k)
                            act.activation(nt_s[s][:, :, :].rearrange("p a f -> p (a f)"), ffn[s][:, 0:256],
                                           ACT.Copy).then_inc(turned_in, 1)

                        def first_gelu(t, k):
                            s = k % 2
                            t.wait(mixed, k)
                            act.activation(g1[s][:, :, :].rearrange("p a f -> p (a f)"), ffn[s][:, 256:512],
                                           ACT.Gelu, bias=bp1[:, 0:1]).then_inc(gelu1, 1)

                        def second_gelu(t, k):
                            s = k % 2
                            t.wait(mixed2, k)
                            t.wait(multiplied, k - 2)
                            act.activation(g2[s][:, :, :].rearrange("p a f -> p (a f)"), ffo[s][:, 0:WT * D],
                                           ACT.Gelu).then_inc(gelu2, 1)

                        def sums_to_sbuf(t, k):
                            t.wait(totalled, k)
                            t.wait_slot(scattered, k - 2, 16 * WT)
                            act.activation(ms[k % 2][:, :, :],
                                           sums[k % 2][:, 0:WT * (D + 1)].rearrange("p (a f) -> p a f", a=WT)[:, :, 0:D],
                                           ACT.Copy).then_inc(copied, 1)

                        def body(t, k):
                            here, last = t.j is not None or k < NWIN, t.j is not None or k > 0
                            if here and n == 1:
                                neighbours_to_sbuf(t, k)
                            if here:
                                rows_to_sbuf(t, k)
                            if here and n == 1:
                                first_gelu(t, k)
                            if last:
                                sums_to_sbuf(t, k - 1)
                            if here and n == 1:
                                second_gelu(t, k)

                        run_turns(act, 2, 0, 2, NWIN // 2 - 1, NWIN, body, range(-1, 4), ((0, 16 * WT), (1, 16 * WT)))

                    @block.vector
                    def _(dve):
                        for s in range(2):
                            dve.memset(part[s][0][:, :, D:D + 2], 1.0)

                        def compare(t, k):
                            s = k % 2
                            t.wait(rows_in, k)
                            t.wait_slot(win_in, k, 16)
                            t.wait(summed, k - 2)
                            for b in range(WT):
                                last = dve.tensor_scalar(eq[s][:, b * WE:(b + 1) * WE], rows[s][:, :], win[s][:, b:b + 1], None,
                                                         ALU.is_equal)
                            last.then_inc(compared, 1)
                            t.wait(indexed, k - 2)
                            dve.tensor_tensor(shift[s][:, :], win[s][:, 0:WT], trash[:, :], ALU.subtract).then_inc(shifted, 1)
                            t.wait(compared, k)
                            t.wait(counted, k - 1)
                            own = eq[s][:, :].rearrange("p (b e) -> p b e", b=WT)[:, :, 0:P]
                            lower = earlier_b[:, :].rearrange("p (o e) -> p o e", o=1).to_broadcast([P, WT, P])
                            dve.tensor_tensor(masked[:, :, :], own, lower, ALU.mult).then_inc(masked_in, 1)
                            t.wait(masked_in, k)
                            dve.tensor_reduce(before[s][:, :], masked[:, :, :], AX_X, ALU.add).then_inc(counted, 1)

                        def message(t, k):
                            s = k % 2
                            if n == 0:
                                t.wait_slot(gathered, k, 16 * WT)
                                of = xg[s]
                            else:
                                t.wait(gelu2, k)
                                of = g2[s]
                            t.wait_slot(win_in, k, 16)
                            t.wait(messaged, k - 1)
                            wb = win[s][:, WT:2 * WT].rearrange("p (b o) -> p b o", o=1).to_broadcast([P, WT, D])
                            dve.tensor_tensor(m[:, :, :], of[:, :, :], wb, ALU.mult).then_inc(multiplied, 1)
                            cut = [part[s][q][:, :, 0:D] for q in range(3)]
                            t.wait(multiplied, k)
                            t.wait(summed, k - 2)
                            dve.tensor_copy(cut[0], m[:, :, :]).then_inc(part0, 1)
                            t.wait(part0, k)
                            dve.tensor_tensor(m[:, :, :], m[:, :, :], cut[0], ALU.subtract).then_inc(rest1, 1)
                            t.wait(rest1, k)
                            dve.tensor_copy(cut[1], m[:, :, :]).then_inc(part1, 1)
                            t.wait(part1, k)
                            dve.tensor_tensor(cut[2], m[:, :, :], cut[1], ALU.subtract).then_inc(messaged, 1)

                        def index(t, k):
                            s = k % 2
                            t.wait(summed, k)
                            t.wait(counted, k)
                            got = sums[s][:, 0:WT * (D + 1)].rearrange("p (a f) -> p a f", a=WT)[:, 1:WT, D]
                            dve.tensor_tensor(before[s][:, 1:WT], before[s][:, 1:WT], got, ALU.add).then_inc(totalled, 1)
                            t.wait(totalled, k)
                            t.wait(shifted, k)
                            dve.scalar_tensor_tensor(out=shift[s][:, :], in0=before[s][:, :], scalar=0.0, in1=shift[s][:, :],
                                                     op0=ALU.is_equal, op1=ALU.mult).then_inc(gated, 1)
                            t.wait(gated, k)
                            t.wait_slot(scattered, k - 2, 16 * WT)
                            dve.tensor_tensor(sidx[s][:, :], shift[s][:, :], trash[:, :], ALU.add).then_inc(indexed, 1)

                        def body(t, k):
                            here, last = t.j is not None or k < NWIN, t.j is not None or k > 0
                            if here and n == 0:
                                message(t, k)
                            if here:
                                compare(t, k)
                            if last:
                                index(t, k - 1)
                            if here and n == 1:
                                message(t, k)

                        run_turns(dve, 2, 0, 2, NWIN // 2 - 1, NWIN, body, range(-1, 4),
                                  ((0, 16 * WT), (1, 16 * WT), (2, 16 * WT), (2, 16)))

        def dense_phase(n):
            x_in, table_out = (x, x1) if n == 0 else (x1, out)
            c = ExitStack()
            with c:
                S = 6
                GF = 4
                sums_of = agg[n][0:N, :]
                pair = [sb(f"pair{n}_{s}", [P, G, 2, D], F32, c) for s in range(S)]
                xs = [sb(f"xs{n}_{s}", [P, G, D], F32, c)[:, :, :] if n == 0 else pair[s][:, :, 0, :] for s in range(S)]
                y = [sb(f"y{n}_{s}", [P, G, D], F32, c) for s in range(S)]
                small = {q: [sb(f"{q}{n}_{s}", [P, G], F32, c) for s in range(S)]
                         for q in ("ssq", "inv", "mean", "var", "rstd")}
                mhalf = sb(f"mhalf{n}", [P, G], F32, c)
                sq_a, sq_b = (sb(f"sq_{q}{n}", [P, G, D], F32, c) for q in "ab")
                turned_s = [[sb(f"turned_s{n}_{s}_{h}", [P, GH * P], F32, c) for h in range(2)] for s in range(2)]
                turned_p = [pb(f"turned_p{n}_{h}", c) for h in range(2)]
                if n == 0:
                    relu = [sb(f"relu_{h}", [P, GH, 2 * D], F32, c) for h in range(2)]
                    zp = [c.enter_context(nc.psum_tensor(f"zp{h}", [P, GH, 256], F32)) for h in range(2)]
                else:
                    hid_s = [sb(f"hid_s{s}", [P, GH * P], F32, c) for s in range(2)]
                    hid_p = [pb(f"hid_p{s}", c) for s in range(2)]
                    out_p = [pb(f"out_p{s}", c) for s in range(2)]

                loads = [sem(f"loads{n}_{s}") for s in range(S)]
                stores = [sem(f"stores{n}_{s}") for s in range(S)]
                mhalf_in = sem(f"mhalf_in{n}")
                passed = sem(f"passed_d{n}")
                two = lambda name: [sem(f"{name}{n}_{h}") for h in range(2)]
                turned = two("turned_d")
                turned_in = two("turned_in_d")
                (squared, ssq_in, ssq_ready, inv_ready, scaled, added, added_dve, mean_in, centred, squared2, var_in, var_ready,
                 rstd_ready, normed) = (sem(f"{q}{n}") for q in (
                     "squared", "ssq_in", "ssq_ready", "inv_ready", "scaled", "added", "added_dve", "mean_in", "centred", "squared2",
                     "var_in", "var_ready", "rstd_ready", "normed"))
                if n == 0:
                    product = sem("product")
                    z_up, relu_in, half_added, y_half = two("z_up"), two("relu_in"), two("half_added"), two("y_half")
                    y_made = y_half[1]
                else:
                    hid_up = two("hid_up")
                    hid_in = sem("hid_in")
                    out_up = sem("out_up")
                    y_made = sem("y_made")
                START = S
                TURNS = (NCH - START - 4) // S

                def run_steps(eng, steps, counts, laps):
                    def body(t, k):
                        for what, behind in steps:
                            if t.j is not None or 0 <= k - behind < NCH:
                                what(t, k - behind)

                    run_turns(eng, S, min(b for _, b in steps), START, TURNS, NCH - 1 + max(b for _, b in steps), body,
                              counts, laps)

                def wide(t):
                    return t[:, :].rearrange("p (g o) -> p g o", o=1).to_broadcast([P, G, D])

                def flat(t):
                    return t.rearrange("p g f -> p (g f)")

                with nc.Block() as block:
                    @block.sync
                    def _(sp):
                        def rows_of(table, t, k):
                            at = t.at(k, CR)
                            if t.j is None and k == NCH - 1:
                                return table[at:at + TAIL, :].rearrange("(p g) f -> p g f", g=TG), TP, TG
                            return table[bass.ds(at, CR), :].rearrange("(p g) f -> p g f", g=G), P, G

                        def load(t, k):
                            s = k % S
                            xr, p, g = rows_of(x_in, t, k)
                            ar, p, g = rows_of(sums_of, t, k)
                            t.wait(added, k - S)
                            t.wait(added_dve, k - S)
                            for h in range(2):
                                t.wait(turned[h], k - S)
                            sp.dma_start(xs[s][0:p, 0:g, :], xr).then_inc(loads[s], 16)
                            sp.dma_start(pair[s][0:p, 0:g, 1, :], ar).then_inc(loads[s], 16)

                        def store(t, k):
                            s = k % S
                            to, p, g = rows_of(table_out, t, k)
                            t.wait(normed, k)
                            sp.dma_start(to, y[s][0:p, 0:g, :]).then_inc(stores[s], 16)

                        run_steps(sp, ((load, -3), (store, 5)), range(START - 5, START + S + 3 - S), ())
                        for s in range(S):
                            sp.wait_ge(stores[s], 16 * len(range(s, NCH, S)))

                    @block.gpsimd
                    def _(pool):
                        pool.memset(mhalf[:, :], -0.5).then_inc(mhalf_in, 1)
                        pool.wait_ge(mhalf_in, 1)

                        def add(t, k):
                            s = k % S
                            t.wait(scaled, k)
                            pool.tensor_tensor(y[s][:, GF:G, :], y[s][:, GF:G, :], xs[s][:, GF:G, :], ALU.add).then_inc(added, 1)

                        def multiply(t, k):
                            s = k % S
                            t.wait_slot(loads, k, 32)
                            for h in range(2):
                                t.wait(turned[h], k - S)
                            pool.tensor_tensor(pair[s][:, :, 0, :], xs[s], pair[s][:, :, 1, :], ALU.mult
                                               ).then_inc(product, 1)

                        def inverse_norm(t, k):
                            t.wait(ssq_ready, k)
                            pool.tensor_tensor(small["inv"][k % S][:, :], small["ssq"][k % S][:, :], mhalf[:, :], ALU.pow
                                               ).then_inc(inv_ready, 1)

                        def inverse_deviation(t, k):
                            t.wait(var_ready, k)
                            pool.tensor_tensor(small["rstd"][k % S][:, :], small["var"][k % S][:, :], mhalf[:, :], ALU.pow
                                               ).then_inc(rstd_ready, 1)

                        if n == 0:
                            run_steps(pool, ((add, 3), (inverse_norm, 2), (multiply, -2), (inverse_deviation, 4)),
                                      range(START - 4, START + S), ((2, 32), (3, 32)))
                        else:
                            run_steps(pool, ((inverse_norm, 2), (inverse_deviation, 4), (add, 2)),
                                      range(START - 4, START + S - 2), ())

                    @block.tensor
                    def _(pe):
                        def transpose_half(h):
                            def step(t, k):
                                s = k % S
                                if n == 0:
                                    t.wait(product, k)
                                else:
                                    t.wait_slot(loads, k, 32)
                                t.wait(turned_in[h], k - 1)
                                for g in range(GH):
                                    last = pe.transpose(turned_p[h][:, g * P:(g + 1) * P], pair[s][:, h * GH + g, :, :].rearrange("p a f -> p (a f)"),
                                                        ident[:, :])
                                last.then_inc(turned[h], 1)
                            return step

                        def products_half(h):
                            def step(t, k):
                                t.wait(turned_in[h], k)
                                t.wait(half_added[h], k - 1)
                                for g in range(0, GH, 2):
                                    pe.matmul(zp[h][:, g:g + 2, 0:3 * D], ones3[:, :],
                                              bias0.rearrange("p (g f) -> p g f", g=2), start=True, stop=False)
                                    for e in range(2):
                                        last = pe.matmul(zp[h][:, g + e, 0:3 * D],
                                                         turned_s[k % 2][h][:, (g + e) * P:(g + e + 1) * P], wz[:, :],
                                                         start=False, stop=(e == 1))
                                last.then_inc(z_up[h], 1)
                            return step

                        def hidden_half(h):
                            def step(t, k):
                                t.wait(turned_in[h], k)
                                t.wait(hid_in, k - 2)
                                pe.matmul(hid_p[k % 2][h * D:(h + 1) * D, :], wu1[:, :], turned_s[k % 2][h][:, :],
                                          start=True, stop=True).then_inc(hid_up[h], 1)
                            return step

                        def outputs(t, k):
                            t.wait(hid_in, k)
                            t.wait(y_made, k - 2)
                            pe.matmul(out_p[k % 2][:, :], ones3[:, :], bias2, start=True, stop=False)
                            to = out_p[k % 2][:, :].rearrange("p (h g f) -> p h g f", h=2, g=GH)
                            for g in range(GH):
                                last = pe.matmul(to[:, :, g, :], hid_s[k % 2][:, g * P:(g + 1) * P], wu2[:, :],
                                                 start=False, stop=(g == GH - 1))
                            last.then_inc(out_up, 1)

                        if n == 0:
                            run_steps(pe, ((products_half(0), 0), (transpose_half(1), -2), (transpose_half(0), -1),
                                           (products_half(1), -1)), range(START - 1, START + S + 2), ())
                        else:
                            run_steps(pe, ((hidden_half(0), 0), (transpose_half(0), -1), (transpose_half(1), -2),
                                           (outputs, 0), (hidden_half(1), -1)),
                                      range(START - 2, START + S + 1), ((2, 32), (3, 32)))

                    @block.scalar
                    def _(act):
                        if n == 1:
                            act.activation(hid_s[0][:, 0:1], ident[:, 0:1], ACT.Gelu).then_inc(passed, 1)
                            act.wait_ge(passed, 1)

                        def turned_to_sbuf(h):
                            def step(t, k):
                                t.wait(turned[h], k)
                                t.wait(z_up[h] if n == 0 else hid_up[h], k - 2)
                                act.activation(turned_s[k % 2][h][:, :], turned_p[h][:, :], ACT.Copy).then_inc(turned_in[h], 1)
                            return step

                        def relus(h):
                            def step(t, k):
                                t.wait(z_up[h], k)
                                t.wait(y_half[h], k - 1)
                                act.activation(relu[h][:, :, :], zp[h][:, :, 0:2 * D], ACT.Relu, scale=1.0 - SLOPE
                                               ).then_inc(relu_in[h], 1)
                            return step

                        def gelu_hidden(t, k):
                            for h in range(2):
                                t.wait(hid_up[h], k)
                            t.wait(out_up, k - 2)
                            act.activation(hid_s[k % 2][:, :], hid_p[k % 2][:, :], ACT.Gelu, bias=bu1[:, 0:1]
                                           ).then_inc(hid_in, 1)

                        def gelu_out(t, k):
                            t.wait(out_up, k)
                            t.wait_slot(stores, k - S, 16)
                            act.activation(flat(y[k % S][:, :, :]), out_p[k % 2][:, :], ACT.Gelu).then_inc(y_made, 1)

                        def square(t, k):
                            if n == 0:
                                t.wait(y_half[0], k)
                            t.wait(y_made, k)
                            t.wait(ssq_in, k - 1)
                            act.activation(sq_a[:, :, :], y[k % S][:, :, :], ACT.Square).then_inc(squared, 1)

                        def square_centred(t, k):
                            t.wait(centred, k)
                            t.wait(var_in, k - 1)
                            act.activation(sq_b[:, :, :], y[k % S][:, :, :], ACT.Square, scale=D ** -0.5
                                           ).then_inc(squared2, 1)

                        if n == 0:
                            run_steps(act, ((square, 2), (relus(1), 1), (square_centred, 4), (relus(0), 1),
                                            (turned_to_sbuf(0), 0), (turned_to_sbuf(1), -1)),
                                      range(START - 5, START + S + 1), ())
                        else:
                            run_steps(act, ((gelu_hidden, 1), (turned_to_sbuf(0), 0), (square_centred, 4),
                                            (turned_to_sbuf(1), -1), (gelu_out, 1), (square, 1)),
                                      range(START - 5, START + S + 1), ((0, 16), (1, 16)))

                    @block.vector
                    def _(dve):
                        def halves(h):
                            return slice(h * GH, (h + 1) * GH)

                        def first_add(h):
                            def step(t, k):
                                t.wait(relu_in[h], k)
                                t.wait_slot(stores, k - S, 16)
                                dve.tensor_tensor(y[k % S][:, halves(h), :], relu[h][:, :, 0:D], zp[h][:, :, 2 * D:3 * D], ALU.add
                                                  ).then_inc(half_added[h], 1)
                            return step

                        def second_add(h):
                            def step(t, k):
                                yh = y[k % S][:, halves(h), :]
                                t.wait(half_added[h], k)
                                dve.tensor_tensor(yh, yh, relu[h][:, :, D:2 * D], ALU.add).then_inc(y_half[h], 1)
                            return step

                        def sum_squares(t, k):
                            t.wait(squared, k)
                            dve.tensor_reduce(small["ssq"][k % S][:, :], sq_a[:, :, :], AX_X, ALU.add).then_inc(ssq_in, 1)

                        def guard_squares(t, k):
                            ssq = small["ssq"][k % S]
                            t.wait(ssq_in, k)
                            dve.tensor_scalar(ssq[:, :], ssq[:, :], L2_EPS, None, ALU.max).then_inc(ssq_ready, 1)

                        def scale(t, k):
                            s = k % S
                            t.wait(inv_ready, k)
                            dve.tensor_tensor(y[s][:, GF:G, :], y[s][:, GF:G, :],
                                              small["inv"][s][:, GF:G].rearrange("p (g o) -> p g o", o=1).to_broadcast([P, G - GF, D]),
                                              ALU.mult).then_inc(scaled, 1)
                            for g in range(GF):
                                last = dve.scalar_tensor_tensor(out=y[s][:, g, :], in0=y[s][:, g, :], scalar=small["inv"][s][:, g:g + 1],
                                                                in1=xs[s][:, g, :], op0=ALU.mult, op1=ALU.add)
                            last.then_inc(added_dve, 1)

                        def mean(t, k):
                            s = k % S
                            t.wait(added, k)
                            t.wait(added_dve, k)
                            dve.tensor_reduce(small["mean"][s][:, :], y[s][:, :, :], AX_X, ALU.add).then_inc(mean_in, 1)

                        def centre(t, k):
                            s = k % S
                            t.wait(mean_in, k)
                            dve.scalar_tensor_tensor(out=y[s][:, :, :], in0=wide(small["mean"][s]), scalar=-1.0 / D,
                                                     in1=y[s][:, :, :], op0=ALU.mult, op1=ALU.add).then_inc(centred, 1)

                        def variance(t, k):
                            t.wait(squared2, k)
                            dve.tensor_reduce(small["var"][k % S][:, :], sq_b[:, :, :], AX_X, ALU.add).then_inc(var_in, 1)

                        def guard_variance(t, k):
                            var = small["var"][k % S]
                            t.wait(var_in, k)
                            dve.tensor_scalar(var[:, :], var[:, :], LN_EPS, None, ALU.add).then_inc(var_ready, 1)

                        def normalize(t, k):
                            s = k % S
                            t.wait(rstd_ready, k)
                            dve.tensor_tensor(y[s][:, :, :], y[s][:, :, :], wide(small["rstd"][s]), ALU.mult
                                              ).then_inc(normed, 1)

                        if n == 0:
                            run_steps(dve, ((second_add(1), 1), (scale, 2), (sum_squares, 1), (normalize, 5), (first_add(1), 0),
                                            (guard_squares, 1), (variance, 3), (mean, 2), (guard_variance, 3),
                                            (first_add(0), 0), (centre, 2), (second_add(0), 0)),
                                      range(START - 5, START + S), ((1, 16),))
                        else:
                            run_steps(dve, ((centre, 3), (scale, 2), (guard_squares, 1), (normalize, 5), (variance, 3),
                                            (mean, 2), (guard_variance, 3), (sum_squares, 0)),
                                      range(START - 5, START + S), ())

        edge_phase(0, x, agg[0])
        dense_phase(0)
        edge_phase(1, x1, agg[1])
        dense_phase(1)


_INS = ['x', 'src', 'dst', 'edge_weight', 'L0_gnn_W1', 'L0_gnn_W2', 'L0_gnn_b1', 'L0_gnn_b2', 'L1_gnn_W1p', 'L1_gnn_b1p',
        'L1_gnn_W2p', 'L1_gnn_b2p', 'L1_gnn_W1u', 'L1_gnn_b1u', 'L1_gnn_W2u', 'L1_gnn_b2u']


def kernel(**inputs):
    import numpy as _np
    import concourse.bacc as _bacc
    from concourse import mybir as _mybir
    from concourse.bass_utils import run_bass_kernel_spmd as _run

    nc = _bacc.Bacc("TRN2", target_bir_lowering=False, num_devices=1)
    arrays, args = {}, []
    for name in _INS:
        a = _np.ascontiguousarray(inputs[name])
        arrays[f"in_{name}"] = a
        args.append(nc.dram_tensor(f"in_{name}", a.shape, _mybir.dt.from_np(a.dtype), kind="ExternalInput").ap())
    args.append(nc.dram_tensor("out_0", arrays["in_x"].shape, _mybir.dt.float32, kind="ExternalOutput").ap())
    gnn_kernel(nc, *args)
    r = _run(nc, [arrays], core_ids=[0])
    return r.results[0]["out_0"]
```

```python
import numpy as np
import concourse.bass as bass
from concourse import mybir
from contextlib import ExitStack

F32 = mybir.dt.float32
BF16 = mybir.dt.bfloat16
I32 = mybir.dt.int32
ALU = mybir.AluOpType
ACT = mybir.ActivationFunctionType
AX_X = mybir.AxisListType.X

P = 128
D = 64
WT = 4
WE = WT * P
G = 8
CR = P * G
FW = G * D
GH = G // 2
L2_EPS = 1e-12
LN_EPS = 1e-5
SLOPE = 0.2
AHEAD = 20
SLOWLY = 14


class Turns:

    def __init__(self, eng, per, j=None, counts=(), laps=()):
        self.eng, self.per, self.j = eng, per, j
        if j is not None:
            self.count = {k: eng.snap(j * per + (k + 1)) for k in counts}
            self.lap = {(n, times): eng.snap(j * times + n * times) for n, times in laps}

    def wait(self, sem, k):
        if self.j is not None:
            self.eng.wait_ge(sem, self.count[k])
        elif k >= 0:
            self.eng.wait_ge(sem, k + 1)

    def wait_slot(self, sems, k, times, since=0):
        n = (k - since) // self.per + 1
        if self.j is not None:
            self.eng.wait_ge(sems[k % self.per], self.lap[n, times])
        elif n > 0:
            self.eng.wait_ge(sems[k % self.per], n * times)

    def at(self, k, size):
        return k * size if self.j is None else self.eng.snap(self.j * (self.per * size) + k * size)


def run_turns(eng, per, first, start, turns, last, body, counts=(), laps=()):
    for k in range(first, start):
        body(Turns(eng, per), k)
    with eng.Fori(0, turns) as j:
        t = Turns(eng, per, j, counts, laps)
        for k in range(start, start + per):
            body(t, k)
    for k in range(start + turns * per, last + 1):
        body(Turns(eng, per), k)


def gnn_kernel(nc, x, src, dst, edge_weight, w1a, w2a, b1a, b2a, w1p, b1p, w2p, b2p, w1u, b1u, w2u, b2u, out):
    N = x.shape[0]
    E = src.shape[0]
    EC = E // P
    ER = E - EC * P
    NWIN = 2 * -(-E // (2 * WE))
    TILES = NWIN * WT
    assert TILES > EC
    NCH = -(-N // CR)
    TAIL = N - (NCH - 1) * CR
    TG = next(g for g in range(G, 0, -1) if TAIL % g == 0 and TAIL // g <= P)
    TP = TAIL // TG
    TRASH = N + 1
    AROWS = P * -(-(TRASH + WE) // P)
    EXTRA = next(p for p in range(P, 0, -1) if (AROWS - N) % p == 0)
    ZC = AROWS // P * D
    ZPARTS = next(z for z in range(20, 200) if ZC % z == 0)

    x1 = nc.dram_tensor("x1", (N, D), F32, kind="Internal").ap()
    agg = [nc.dram_tensor(f"agg{n}", (AROWS, D), F32, kind="Internal").ap() for n in range(2)]

    ctx = ExitStack()
    with ctx:
        def sb(name, shape, dt=F32, c=ctx):
            return c.enter_context(nc.sbuf_tensor(name, shape, dt))

        def pb(name, c):
            return c.enter_context(nc.psum_tensor(name, [P, 512], F32))

        def sem(name, c=ctx):
            return c.enter_context(nc.semaphore(name))

        gather_idx = [sb(f"gather_idx{n}", [P, TILES], I32) for n in range(2)]
        scatter_raw = [sb(f"scatter_raw{n}", [P, TILES], I32) for n in range(2)]
        ew = sb("ew", [P, TILES])
        sw = [sb(f"sw{n}", [P, NWIN, 2 * WT]) for n in range(2)]
        ident = sb("ident", [P, P])
        earlier = sb("earlier", [P, P])
        earlier_b = sb("earlier_b", [P, P], BF16)
        trash_i = sb("trash_i", [P, WT], I32)
        trash = sb("trash", [P, WT])
        ones3 = sb("ones3", [P, P], BF16)
        wz = sb("wz", [P, 3 * D])
        wp1 = sb("wp1", [P, P])
        wp2 = sb("wp2", [P, P])
        wu1 = sb("wu1", [P, D])
        wu2 = sb("wu2", [P, P])
        bp1 = sb("bp1", [P, 1])
        bu1 = sb("bu1", [P, 1])
        NB0, NB1, NB2 = 2 * 3 * D, WT * D, G * D
        NB = NB0 + NB1 + NB2
        brow = sb("brow", [1, NB])
        brest = sb("brest", [1, NB])
        bparts = sb("bparts", [1, 3, NB], BF16)
        bias = sb("bias", [P, NB], BF16)
        bias0, bias1, bias2 = bias[:, 0:NB0], bias[:, NB0:NB0 + NB1], bias[:, NB0 + NB1:NB]
        zeros = sb("zeros", [P, max(ZC // ZPARTS, FW)])

        loaded = sem("loaded")
        prepared = sem("prepared")
        made = sem("made")
        weights_in = sem("weights_in")
        chain = sem("chain")
        split_done = sem("split_done")
        zeroed0 = [sem(f"zeroed0_{s}") for s in range(2)]
        zeroed1 = sem("zeroed1")
        zeros_made = sem("zeros_made")

        table_loads, weight_loads = [], []
        for t, s in ((gather_idx[0], src), (scatter_raw[0], dst), (ew, edge_weight), (gather_idx[1], dst), (scatter_raw[1], src)):
            table_loads.append((t[:, 0:EC], s[0:EC * P].rearrange("(p t) -> p t", p=P)))
            if ER:
                table_loads.append((t[0:ER, EC:EC + 1], s[EC * P:E].rearrange("(p t) -> p t", t=1)))
        for t, w in ((wp1, w1p), (wp2, w2p), (wu2, w2u)):
            weight_loads += [(t[0:D, 0:D], w), (t[D:2 * D, D:2 * D], w)]
        weight_loads += [(wz[0:D, 0:D], w1a), (wz[D:2 * D, D:2 * D], w2a),
                         (wz[0:D, 2 * D:3 * D], w1a), (wz[D:2 * D, 2 * D:3 * D], w2a), (wu1[:, :], w1u)]
        for t, b in ((bp1, b1p), (bu1, b1u)):
            for h in range(2):
                weight_loads.append((t[h * D:(h + 1) * D, 0:1], b.rearrange("(f o) -> f o", o=1)))
        for h in range(2):
            weight_loads += [(brow[0:1, (3 * h) * D:(3 * h + 1) * D], b1a), (brow[0:1, (3 * h + 1) * D:(3 * h + 2) * D], b2a)]
        for at, times, b in ((NB0, WT, b2p), (NB0 + NB1, G, b2u)):
            for g in range(times):
                weight_loads.append((brow[0:1, at + g * D:at + (g + 1) * D], b.rearrange("(o f) -> o f", o=1)))
        N_TABLES, N_WEIGHTS = 16 * len(table_loads), 16 * len(weight_loads)

        with nc.Block() as block:
            @block.vector
            def _(dve):
                dve.memset(zeros[:, :], 0.0).then_inc(zeros_made, 1)
                for t, pad in ((gather_idx[0], 0), (gather_idx[1], 0), (scatter_raw[0], N), (scatter_raw[1], N)):
                    dve.memset(t[:, EC:TILES], pad)
                dve.memset(ew[:, EC:TILES], 0.0).then_inc(prepared, 1)
                dve.memset(ones3[:, :], 0.0).then_inc(prepared, 1)
                dve.wait_ge(prepared, 2)
                dve.memset(ones3[0:3, :], 1.0)
                dve.wait_ge(made, 4)
                dve.tensor_copy(trash[:, :], trash_i[:, :])
                dve.tensor_copy(earlier_b[:, :], earlier[:, :])
                dve.wait_ge(loaded, N_TABLES)
                for n in range(2):
                    dve.tensor_copy(sw[n][:, :, 0:WT], scatter_raw[n][:, :].rearrange("p (k b) -> p k b", b=WT))
                    dve.tensor_copy(sw[n][:, :, WT:2 * WT], ew[:, :].rearrange("p (k b) -> p k b", b=WT))

            @block.gpsimd
            def _(pool):
                pool.memset(ident[:, :], 0.0).then_inc(made, 1)
                pool.memset(earlier[:, :], 1.0).then_inc(made, 1)
                pool.wait_ge(made, 2)
                pool.affine_select(out=ident[:, :], in_=ident[:, :], compare_op=ALU.not_equal, fill=1.0, base=0,
                                   pattern=[[-1, P]], channel_multiplier=1)
                pool.affine_select(out=earlier[:, :], in_=earlier[:, :], compare_op=ALU.is_gt, fill=0.0, base=0,
                                   pattern=[[-1, P]], channel_multiplier=1).then_inc(made, 1)
                pool.iota(trash_i[:, :], pattern=[[P, WT]], base=TRASH, channel_multiplier=1).then_inc(made, 1)

            @block.sync
            def _(sp):
                sp.wait_ge(prepared, 1)
                for to, of in table_loads:
                    sp.dma_start(to, of).then_inc(loaded, 16)
                sp.wait_ge(loaded, N_TABLES)

        def edge_phase(n, table_in, table_out):
            c = ExitStack()
            with c:
                idx = [sb(f"idx{n}_{s}", [P, WT], I32, c) for s in range(2)]
                win = [sb(f"win{n}_{s}", [P, 2 * WT], F32, c) for s in range(2)]
                xg = [sb(f"xg{n}_{s}", [P, WT, D], F32, c) for s in range(2)]
                assert SLOWLY <= AHEAD - 2
                PRE = min(AHEAD + SLOWLY, NWIN - 4) if n == 0 else 0
                if PRE:
                    xg_pre = sb("xg_pre", [P, PRE, WT, D], F32, c)
                    gathered_pre = [sem(f"gathered_pre{q}") for q in range(-(-PRE // 4))]
                START = PRE + 2 if PRE else 4
                m = sb(f"m{n}", [P, WT, D], F32, c)
                part = [[sb(f"part{n}_{q}_{s}", [P, WT, D + 2], BF16, c) for q in range(3)] for s in range(2)]
                rows = [sb(f"rows{n}_{s}", [P, WE], F32, c) for s in range(2)]
                eq = [sb(f"eq{n}_{s}", [P, WT * (WE + P)], BF16, c) for s in range(2)]
                ms = [sb(f"ms{n}_{s}", [P, WT, D], F32, c) for s in range(2)]
                before = [sb(f"before{n}_{s}", [P, WT], F32, c) for s in range(2)]
                shift = [sb(f"shift{n}_{s}", [P, WT], F32, c) for s in range(2)]
                sidx = [sb(f"sidx{n}_{s}", [P, WT], I32, c) for s in range(2)]
                masked = sb(f"masked{n}", [P, WT, P], BF16, c)
                rowp = [pb(f"rowp{n}_{s}", c) for s in range(2)]
                sums = [pb(f"sums{n}_{s}", c) for s in range(2)]
                if n == 1:
                    nt_s = [sb(f"nt_s{s}", [P, 2, P], F32, c) for s in range(2)]
                    g1 = [sb(f"g1_{s}", [P, 2, P], F32, c) for s in range(2)]
                    g2 = [sb(f"g2_{s}", [P, WT, D], F32, c) for s in range(2)]
                    ffn = [pb(f"ffn{s}", c) for s in range(2)]
                    ffo = [pb(f"ffo{s}", c) for s in range(2)]

                idx_in = [sem(f"idx_in{n}_{s}") for s in range(2)]
                win_in = [sem(f"win_in{n}_{s}") for s in range(2)]
                gathered = [sem(f"gathered{n}_{s}") for s in range(2)]
                scattered = [sem(f"scattered{n}_{s}") for s in range(2)]
                rows_up = sem(f"rows_up{n}")
                rows_in = sem(f"rows_in{n}")
                compared = sem(f"compared{n}")
                counted = sem(f"counted{n}")
                messaged = sem(f"messaged{n}")
                summed = sem(f"summed{n}")
                copied = sem(f"copied{n}")
                indexed = sem(f"indexed{n}")
                shifted, masked_in, totalled, gated, multiplied, rest1, part0, part1 = (sem(f"{q}{n}") for q in (
                    "shifted", "masked_in", "totalled", "gated", "multiplied", "rest1_", "part0_", "part1_"))
                preset = sem(f"preset{n}")
                passed = sem(f"passed{n}")
                if n == 1:
                    turned = sem("turned")
                    turned_in = sem("turned_in")
                    mixed = sem("mixed")
                    gelu1 = sem("gelu1")
                    mixed2 = sem("mixed2")
                    gelu2 = sem("gelu2")

                with nc.Block() as block:
                    @block.sync
                    def _(sp):
                        def body(t, k):
                            s = k % 2
                            at = t.at(k, 1)
                            if k >= PRE:
                                at4 = t.at(k, WT)
                                t.wait_slot(gathered, k - 2, 16 * WT, PRE)
                                sp.dma_start(idx[s][:, :], gather_idx[n][:, bass.ds(at4, WT)]).then_inc(idx_in[s], 16)
                            t.wait(shifted, k - 2)
                            t.wait(multiplied, k - 2)
                            sp.dma_start(win[s][:, :], sw[n][:, bass.ds(at, 1), :].rearrange("p o b -> p (o b)")
                                         ).then_inc(win_in[s], 16)

                        for k in range(2):
                            body(Turns(sp, 2), k)
                        if n == 0:
                            sp.wait_ge(zeros_made, 1)
                            cleared = agg[0].rearrange("(p r) f -> p (r f)", p=P)
                            for z in range(ZPARTS):
                                cut = slice(z * ZC // ZPARTS, (z + 1) * ZC // ZPARTS)
                                if z >= 2:
                                    sp.wait_ge(zeroed0[z % 2], 16 * (z // 2))
                                sp.dma_start(cleared[:, cut], zeros[:, 0:ZC // ZPARTS]).then_inc(zeroed0[z % 2], 16)
                        run_turns(sp, 2, 2, START, (NWIN - START) // 2, NWIN - 1, body, range(START - 2, START),
                                  (((START - PRE) // 2, 16 * WT),))
                        if n == 0:
                            sp.wait_ge(prepared, 3)
                            for to, of in weight_loads:
                                sp.dma_start(to, of).then_inc(weights_in, 16)
                            sp.wait_ge(split_done, 1)
                            for r in range(3):
                                sp.dma_start(bias[r:r + 1, :], bparts[0:1, r, :]).then_inc(weights_in, 16)
                            sp.wait_ge(weights_in, N_WEIGHTS + 48)

                    @block.gpsimd
                    def _(pool):
                        early = [(k, b) for k in range(PRE) for b in range(WT)]

                        def gather_early(tiles):
                            for k, b in tiles:
                                at = k * WT + b
                                pool.indirect_dma_start(
                                    out=xg_pre[:, k, b, :], out_offset=None, in_=table_in[:, :],
                                    in_offset=bass.IndirectOffsetOnAxis(ap=gather_idx[n][:, at:at + 1], axis=0),
                                ).then_inc(gathered_pre[k // 4], 16)

                        def body(t, k):
                            s = k % 2
                            if k < PRE:
                                at = AHEAD * WT + (k - 2) * WT // 2
                                gather_early(early[at:at + WT // 2])
                            if PRE <= k < NWIN or t.j is not None:
                                t.wait_slot(idx_in, k, 16, PRE)
                                t.wait(multiplied if n == 0 else turned, k - 2)
                                pool.sem_inc(passed, 1)
                                for b in range(WT):
                                    pool.indirect_dma_start(
                                        out=xg[s][:, b, :], out_offset=None, in_=table_in[:, :],
                                        in_offset=bass.IndirectOffsetOnAxis(ap=idx[s][:, b:b + 1], axis=0),
                                    ).then_inc(gathered[s], 16)
                            if k >= 2:
                                if k == 2 and n == 0 and t.j is None:
                                    for z in range(2):
                                        pool.wait_ge(zeroed0[z], 16 * len(range(z, ZPARTS, 2)))
                                t.wait(copied, k - 2)
                                t.wait(indexed, k - 2)
                                t.wait_slot(scattered, k - 3, 16 * WT)
                                pool.sem_inc(passed, 1)
                                for b in range(WT):
                                    pool.indirect_dma_start(
                                        out=table_out[:, :],
                                        out_offset=bass.IndirectOffsetOnAxis(ap=sidx[s][:, b:b + 1], axis=0),
                                        in_=ms[s][:, b, :], in_offset=None, compute_op=ALU.add,
                                    ).then_inc(scattered[s], 16)

                        gather_early(early[0:AHEAD * WT])
                        run_turns(pool, 2, 2 if PRE else 0, START, (NWIN - START) // 2, NWIN + 1, body,
                                  range(START - 2, START),
                                  (((START - PRE) // 2 + 1, 16), (START // 2 - 1, 16 * WT), (START // 2, 16 * WT)))
                        for s in range(2):
                            pool.wait_ge(scattered[s], 16 * WT * (NWIN // 2))

                    @block.tensor
                    def _(pe):
                        def spread_rows(t, k):
                            t.wait_slot(win_in, k, 16)
                            t.wait(rows_in, k - 2)
                            for b in range(WT):
                                last = pe.transpose(rowp[k % 2][:, b * P:(b + 1) * P],
                                                    win[k % 2][:, b:b + 1].to_broadcast([P, P]), ident[:, :])
                            last.then_inc(rows_up, 1)

                        def transpose_neighbours(t, k):
                            s = k % 2
                            t.wait_slot(gathered, k, 16 * WT)
                            t.wait(gelu1, k - 2)
                            for q in range(2):
                                last = pe.transpose(ffn[s][:, q * P:(q + 1) * P],
                                                    xg[s][:, 2 * q:2 * q + 2, :].rearrange("p a f -> p (a f)"), ident[:, :])
                            last.then_inc(turned, 1)

                        def first_product(t, k):
                            s = k % 2
                            t.wait(turned_in, k)
                            pe.matmul(ffn[s][:, 256:512], wp1[:, :], nt_s[s][:, :, :].rearrange("p a f -> p (a f)"),
                                      start=True, stop=True).then_inc(mixed, 1)

                        def second_product(t, k):
                            s = k % 2
                            t.wait(gelu1, k)
                            t.wait(gelu2, k - 2)
                            pe.matmul(ffo[s][:, 0:WT * D], ones3[:, :], bias1, start=True, stop=False)
                            for q in range(2):
                                last = pe.matmul(ffo[s][:, q * P:(q + 1) * P], g1[s][:, q, :], wp2[:, :],
                                                 start=False, stop=(q == 1))
                            last.then_inc(mixed2, 1)

                        def add_equal(t, k):
                            s = k % 2
                            t.wait(compared, k)
                            t.wait(messaged, k)
                            t.wait(copied, k - 2)
                            t.wait(indexed, k - 2)
                            for a in range(WT):
                                for b in range(WT):
                                    same = eq[s][:, b * WE + a * P:b * WE + (a + 1) * P]
                                    for q in range(3):
                                        w = D + 1 if b < a and q == 0 else D
                                        last = pe.matmul(sums[s][:, a * (D + 1):a * (D + 1) + w], same,
                                                         part[s][q][:, b, 0:w], start=(b == q == 0),
                                                         stop=(b == WT - 1 and q == 2))
                            last.then_inc(summed, 1)

                        def body(t, k):
                            here, last = t.j is not None or k < NWIN, t.j is not None or k > 0
                            if here and n == 1:
                                transpose_neighbours(t, k)
                            if here:
                                spread_rows(t, k)
                            if here and n == 1:
                                first_product(t, k)
                            if last:
                                add_equal(t, k - 1)
                            if here and n == 1:
                                second_product(t, k)

                        run_turns(pe, 2, 0, START, (NWIN - START) // 2, NWIN, body, range(START - 3, START + 2),
                                  ((START // 2 + 1, 16), (START // 2 + 1, 16 * WT)))

                    @block.scalar
                    def _(act):
                        if n == 1:
                            act.activation(g1[0][:, 0, 0:1], ident[:, 0:1], ACT.Gelu).then_inc(preset, 1)
                            act.wait_ge(preset, 1)

                        def rows_to_sbuf(t, k):
                            t.wait(rows_up, k)
                            t.wait(compared, k - 2)
                            act.activation(rows[k % 2][:, :], rowp[k % 2][:, :], ACT.Copy).then_inc(rows_in, 1)

                        def neighbours_to_sbuf(t, k):
                            s = k % 2
                            t.wait(turned, k)
                            act.activation(nt_s[s][:, :, :].rearrange("p a f -> p (a f)"), ffn[s][:, 0:256],
                                           ACT.Copy).then_inc(turned_in, 1)

                        def first_gelu(t, k):
                            s = k % 2
                            t.wait(mixed, k)
                            act.activation(g1[s][:, :, :].rearrange("p a f -> p (a f)"), ffn[s][:, 256:512],
                                           ACT.Gelu, bias=bp1[:, 0:1]).then_inc(gelu1, 1)

                        def second_gelu(t, k):
                            s = k % 2
                            t.wait(mixed2, k)
                            t.wait(multiplied, k - 2)
                            act.activation(g2[s][:, :, :].rearrange("p a f -> p (a f)"), ffo[s][:, 0:WT * D],
                                           ACT.Gelu).then_inc(gelu2, 1)

                        def sums_to_sbuf(t, k):
                            t.wait(totalled, k)
                            t.wait_slot(scattered, k - 2, 16 * WT)
                            act.activation(ms[k % 2][:, :, :],
                                           sums[k % 2][:, 0:WT * (D + 1)].rearrange("p (a f) -> p a f", a=WT)[:, :, 0:D],
                                           ACT.Copy).then_inc(copied, 1)

                        def body(t, k):
                            here, last = t.j is not None or k < NWIN, t.j is not None or k > 0
                            if here and n == 1:
                                neighbours_to_sbuf(t, k)
                            if here:
                                rows_to_sbuf(t, k)
                            if here and n == 1:
                                first_gelu(t, k)
                            if last:
                                sums_to_sbuf(t, k - 1)
                            if here and n == 1:
                                second_gelu(t, k)

                        run_turns(act, 2, 0, START, (NWIN - START) // 2, NWIN, body, range(START - 3, START + 2),
                                  ((START // 2 - 1, 16 * WT), (START // 2, 16 * WT)))

                    @block.vector
                    def _(dve):
                        for s in range(2):
                            dve.memset(part[s][0][:, :, D:D + 2], 1.0)
                        if n == 0:
                            for t in (wp1, wp2, wu2, wz):
                                dve.memset(t[:, :], 0.0)
                            dve.memset(bias[:, :], 0.0).then_inc(prepared, 1)

                        def prepare_weights():
                            dve.wait_ge(weights_in, N_WEIGHTS)
                            dve.tensor_scalar(wz[:, 2 * D:3 * D], wz[:, 2 * D:3 * D], SLOPE, None, ALU.mult)
                            b0 = brow[0:1, 0:NB0].rearrange("o (h k f) -> o h k f", h=2, k=3)
                            step = 0

                            def link(ins):
                                nonlocal step
                                step += 1
                                ins.then_inc(chain, 1)
                                dve.wait_ge(chain, step)

                            link(dve.tensor_tensor(b0[:, :, 2, :], b0[:, :, 0, :], b0[:, :, 1, :], ALU.add))
                            link(dve.tensor_scalar(b0[:, :, 2, :], b0[:, :, 2, :], SLOPE, None, ALU.mult))
                            link(dve.tensor_copy(bparts[0:1, 0, :], brow[0:1, :]))
                            link(dve.tensor_tensor(brest[0:1, :], brow[0:1, :], bparts[0:1, 0, :], ALU.subtract))
                            link(dve.tensor_copy(bparts[0:1, 1, :], brest[0:1, :]))
                            link(dve.tensor_tensor(brest[0:1, :], brest[0:1, :], bparts[0:1, 1, :], ALU.subtract))
                            dve.tensor_copy(bparts[0:1, 2, :], brest[0:1, :]).then_inc(split_done, 1)

                        def compare(t, k):
                            s = k % 2
                            t.wait(rows_in, k)
                            t.wait_slot(win_in, k, 16)
                            t.wait(summed, k - 2)
                            for b in range(WT):
                                last = dve.tensor_scalar(eq[s][:, b * WE:(b + 1) * WE], rows[s][:, :], win[s][:, b:b + 1], None,
                                                         ALU.is_equal)
                            last.then_inc(compared, 1)
                            t.wait(indexed, k - 2)
                            dve.tensor_tensor(shift[s][:, :], win[s][:, 0:WT], trash[:, :], ALU.subtract).then_inc(shifted, 1)
                            t.wait(compared, k)
                            t.wait(counted, k - 1)
                            own = eq[s][:, :].rearrange("p (b e) -> p b e", b=WT)[:, :, 0:P]
                            lower = earlier_b[:, :].rearrange("p (o e) -> p o e", o=1).to_broadcast([P, WT, P])
                            dve.tensor_tensor(masked[:, :, :], own, lower, ALU.mult).then_inc(masked_in, 1)
                            t.wait(masked_in, k)
                            dve.tensor_reduce(before[s][:, :], masked[:, :, :], AX_X, ALU.add).then_inc(counted, 1)

                        def message(t, k):
                            s = k % 2
                            if n == 0:
                                if k < PRE:
                                    dve.wait_ge(gathered_pre[k // 4], 16 * WT * min(4, PRE - k // 4 * 4))
                                    of = xg_pre[:, k, :, :]
                                else:
                                    t.wait_slot(gathered, k, 16 * WT, PRE)
                                    of = xg[s][:, :, :]
                            else:
                                t.wait(gelu2, k)
                                of = g2[s][:, :, :]
                            t.wait_slot(win_in, k, 16)
                            t.wait(messaged, k - 1)
                            wb = win[s][:, WT:2 * WT].rearrange("p (b o) -> p b o", o=1).to_broadcast([P, WT, D])
                            dve.tensor_tensor(m[:, :, :], of, wb, ALU.mult).then_inc(multiplied, 1)
                            cut = [part[s][q][:, :, 0:D] for q in range(3)]
                            t.wait(multiplied, k)
                            t.wait(summed, k - 2)
                            dve.tensor_copy(cut[0], m[:, :, :]).then_inc(part0, 1)
                            t.wait(part0, k)
                            dve.tensor_tensor(m[:, :, :], m[:, :, :], cut[0], ALU.subtract).then_inc(rest1, 1)
                            t.wait(rest1, k)
                            dve.tensor_copy(cut[1], m[:, :, :]).then_inc(part1, 1)
                            t.wait(part1, k)
                            dve.tensor_tensor(cut[2], m[:, :, :], cut[1], ALU.subtract).then_inc(messaged, 1)

                        def index(t, k):
                            s = k % 2
                            t.wait(summed, k)
                            t.wait(counted, k)
                            got = sums[s][:, 0:WT * (D + 1)].rearrange("p (a f) -> p a f", a=WT)[:, 1:WT, D]
                            dve.tensor_tensor(before[s][:, 1:WT], before[s][:, 1:WT], got, ALU.add).then_inc(totalled, 1)
                            t.wait(totalled, k)
                            t.wait(shifted, k)
                            dve.scalar_tensor_tensor(out=shift[s][:, :], in0=before[s][:, :], scalar=0.0, in1=shift[s][:, :],
                                                     op0=ALU.is_equal, op1=ALU.mult).then_inc(gated, 1)
                            t.wait(gated, k)
                            t.wait_slot(scattered, k - 2, 16 * WT)
                            dve.tensor_tensor(sidx[s][:, :], shift[s][:, :], trash[:, :], ALU.add).then_inc(indexed, 1)

                        def body(t, k):
                            here, last = t.j is not None or k < NWIN, t.j is not None or k > 0
                            if here and n == 0:
                                message(t, k)
                            if here:
                                compare(t, k)
                            if last:
                                index(t, k - 1)
                            if here and n == 1:
                                message(t, k)

                        run_turns(dve, 2, 0, START, (NWIN - START) // 2, NWIN, body, range(START - 3, START + 2),
                                  ((START // 2 - 1, 16 * WT), (START // 2, 16 * WT), (START // 2 + 1, 16 * WT),
                                   (START // 2 + 1, 16), ((START - PRE) // 2 + 1, 16 * WT)))
                        if n == 0:
                            prepare_weights()

        def dense_phase(n):
            x_in, table_out = (x, x1) if n == 0 else (x1, out)
            c = ExitStack()
            with c:
                S = 6
                GF = 4
                GA = 5 - 2 * n
                sums_of = agg[n][0:N, :]
                pair = [sb(f"pair{n}_{s}", [P, G, 2, D], F32, c) for s in range(S)]
                xs = [sb(f"xs{n}_{s}", [P, G, D], F32, c)[:, :, :] if n == 0 else pair[s][:, :, 0, :] for s in range(S)]
                y = [sb(f"y{n}_{s}", [P, G, D], F32, c) for s in range(S)]
                small = {q: [sb(f"{q}{n}_{s}", [P, G], F32, c) for s in range(S)]
                         for q in ("ssq", "inv", "mean", "var", "rstd")}
                mhalf = sb(f"mhalf{n}", [P, G], F32, c)
                sq_a, sq_b = (sb(f"sq_{q}{n}", [P, G, D], F32, c) for q in "ab")
                turned_s = [[sb(f"turned_s{n}_{s}_{h}", [P, GH * P], F32, c) for h in range(2)] for s in range(2)]
                turned_p = [pb(f"turned_p{n}_{h}", c) for h in range(2)]
                if n == 0:
                    relu = sb("relu", [P, 2, GH, 2 * D], F32, c)
                    zp = [c.enter_context(nc.psum_tensor(f"zp{h}", [P, GH, 256], F32)) for h in range(2)]
                else:
                    hid_s = [sb(f"hid_s{s}", [P, GH * P], F32, c) for s in range(2)]
                    hid_p = [pb(f"hid_p{s}", c) for s in range(2)]
                    out_p = [pb(f"out_p{s}", c) for s in range(2)]

                loads = [sem(f"loads{n}_{s}") for s in range(S)]
                stores = [sem(f"stores{n}_{s}") for s in range(S)]
                mhalf_in = sem(f"mhalf_in{n}")
                passed = sem(f"passed_d{n}")
                two = lambda name: [sem(f"{name}{n}_{h}") for h in range(2)]
                turned = two("turned_d")
                turned_in = two("turned_in_d")
                (squared, ssq_in, ssq_ready, inv_ready, scaled, added, added_dve, mean_in, centred, squared2, var_in, var_ready,
                 rstd_ready, normed, normed_act) = (sem(f"{q}{n}") for q in (
                     "squared", "ssq_in", "ssq_ready", "inv_ready", "scaled", "added", "added_dve", "mean_in", "centred", "squared2",
                     "var_in", "var_ready", "rstd_ready", "normed", "normed_act"))
                if n == 0:
                    product = sem("product")
                    z_up, relu_in, half_added = two("z_up"), two("relu_in"), two("half_added")
                    y_made = sem("y_made0")
                else:
                    hid_up = two("hid_up")
                    hid_in = sem("hid_in")
                    out_up = sem("out_up")
                    y_made = sem("y_made")
                START = S + 1
                TURNS = (NCH - START - 4) // S

                def run_steps(eng, steps, counts, laps):
                    def body(t, k):
                        for what, behind in steps:
                            if t.j is not None or 0 <= k - behind < NCH:
                                what(t, k - behind)

                    run_turns(eng, S, min(b for _, b in steps), START, TURNS, NCH - 1 + max(b for _, b in steps), body,
                              counts, laps)

                def wide(t, first=0):
                    return t[:, first:G].rearrange("p (g o) -> p g o", o=1).to_broadcast([P, G - first, D])

                def flat(t):
                    return t.rearrange("p g f -> p (g f)")

                with nc.Block() as block:
                    @block.sync
                    def _(sp):
                        def rows_of(table, t, k):
                            at = t.at(k, CR)
                            if t.j is None and k == NCH - 1:
                                return table[at:at + TAIL, :].rearrange("(p g) f -> p g f", g=TG), TP, TG
                            return table[bass.ds(at, CR), :].rearrange("(p g) f -> p g f", g=G), P, G

                        def load(t, k):
                            s = k % S
                            xr, p, g = rows_of(x_in, t, k)
                            ar, p, g = rows_of(sums_of, t, k)
                            t.wait(added, k - S)
                            t.wait(added_dve, k - S)
                            for h in range(2):
                                t.wait(turned[h], k - S)
                            sp.dma_start(xs[s][0:p, 0:g, :], xr).then_inc(loads[s], 16)
                            sp.dma_start(pair[s][0:p, 0:g, 1, :], ar).then_inc(loads[s], 16)

                        def store(t, k):
                            s = k % S
                            to, p, g = rows_of(table_out, t, k)
                            t.wait(normed, k)
                            t.wait(normed_act, k)
                            sp.dma_start(to, y[s][0:p, 0:g, :]).then_inc(stores[s], 16)

                        def clear(t, k):
                            to, p, g = rows_of(agg[1], t, k)
                            sp.dma_start(to, zeros[0:p, 0:g * D].rearrange("p (g f) -> p g f", g=g)).then_inc(zeroed1, 16)

                        if n == 0:
                            sp.dma_start(agg[1][N:AROWS, :].rearrange("(p r) f -> p (r f)", p=EXTRA),
                                         zeros[0:EXTRA, 0:(AROWS - N) // EXTRA * D]).then_inc(zeroed1, 16)
                        run_steps(sp, ((load, -3), (store, 5)) + (((clear, 0),) if n == 0 else ()), range(START - 5, START + S + 3 - S), ())
                        for s in range(S):
                            sp.wait_ge(stores[s], 16 * len(range(s, NCH, S)))
                        if n == 0:
                            sp.wait_ge(zeroed1, 16 * (NCH + 1))

                    @block.gpsimd
                    def _(pool):
                        pool.memset(mhalf[:, :], -0.5).then_inc(mhalf_in, 1)
                        pool.wait_ge(mhalf_in, 1)

                        def add(t, k):
                            s = k % S
                            t.wait(scaled, k)
                            pool.tensor_tensor(y[s][:, GF:G, :], y[s][:, GF:G, :], xs[s][:, GF:G, :], ALU.add).then_inc(added, 1)

                        def multiply(t, k):
                            s = k % S
                            t.wait_slot(loads, k, 32)
                            for h in range(2):
                                t.wait(turned[h], k - S)
                            pool.tensor_tensor(pair[s][:, :, 0, :], xs[s], pair[s][:, :, 1, :], ALU.mult
                                               ).then_inc(product, 1)

                        def inverse_norm(t, k):
                            t.wait(ssq_ready, k)
                            pool.tensor_tensor(small["inv"][k % S][:, :], small["ssq"][k % S][:, :], mhalf[:, :], ALU.pow
                                               ).then_inc(inv_ready, 1)

                        def inverse_deviation(t, k):
                            t.wait(var_ready, k)
                            pool.tensor_tensor(small["rstd"][k % S][:, :], small["var"][k % S][:, :], mhalf[:, :], ALU.pow
                                               ).then_inc(rstd_ready, 1)

                        if n == 0:
                            run_steps(pool, ((add, 3), (inverse_norm, 2), (multiply, -2), (inverse_deviation, 4)),
                                      range(START - 4, START + 4), ((2, 32), (3, 32)))
                        else:
                            run_steps(pool, ((inverse_norm, 2), (inverse_deviation, 4), (add, 2)),
                                      range(START - 4, START + S - 2), ())

                    @block.tensor
                    def _(pe):
                        def transpose_half(h):
                            def step(t, k):
                                s = k % S
                                if n == 0:
                                    t.wait(product, k)
                                else:
                                    t.wait_slot(loads, k, 32)
                                t.wait(turned_in[h], k - 1)
                                for g in range(GH):
                                    last = pe.transpose(turned_p[h][:, g * P:(g + 1) * P], pair[s][:, h * GH + g, :, :].rearrange("p a f -> p (a f)"),
                                                        ident[:, :])
                                last.then_inc(turned[h], 1)
                            return step

                        def products_half(h):
                            def step(t, k):
                                t.wait(turned_in[h], k)
                                t.wait(half_added[h], k - 1)
                                for g in range(0, GH, 2):
                                    pe.matmul(zp[h][:, g:g + 2, 0:3 * D], ones3[:, :],
                                              bias0.rearrange("p (g f) -> p g f", g=2), start=True, stop=False)
                                    for e in range(2):
                                        last = pe.matmul(zp[h][:, g + e, 0:3 * D],
                                                         turned_s[k % 2][h][:, (g + e) * P:(g + e + 1) * P], wz[:, :],
                                                         start=False, stop=(e == 1))
                                last.then_inc(z_up[h], 1)
                            return step

                        def hidden_half(h):
                            def step(t, k):
                                t.wait(turned_in[h], k)
                                t.wait(hid_in, k - 2)
                                pe.matmul(hid_p[k % 2][h * D:(h + 1) * D, :], wu1[:, :], turned_s[k % 2][h][:, :],
                                          start=True, stop=True).then_inc(hid_up[h], 1)
                            return step

                        def outputs(t, k):
                            t.wait(hid_in, k)
                            t.wait(y_made, k - 2)
                            pe.matmul(out_p[k % 2][:, :], ones3[:, :], bias2, start=True, stop=False)
                            to = out_p[k % 2][:, :].rearrange("p (h g f) -> p h g f", h=2, g=GH)
                            for g in range(GH):
                                last = pe.matmul(to[:, :, g, :], hid_s[k % 2][:, g * P:(g + 1) * P], wu2[:, :],
                                                 start=False, stop=(g == GH - 1))
                            last.then_inc(out_up, 1)

                        if n == 0:
                            run_steps(pe, ((products_half(0), 0), (transpose_half(1), -2), (transpose_half(0), -1),
                                           (products_half(1), -1)), range(START - 1, START + S + 2), ())
                        else:
                            run_steps(pe, ((hidden_half(0), 0), (transpose_half(0), -1), (transpose_half(1), -2),
                                           (outputs, 0), (hidden_half(1), -1)),
                                      range(START - 2, START + S + 1), ((2, 32), (3, 32)))

                    @block.scalar
                    def _(act):
                        if n == 1:
                            act.activation(hid_s[0][:, 0:1], ident[:, 0:1], ACT.Gelu).then_inc(passed, 1)
                            act.wait_ge(passed, 1)

                        def turned_to_sbuf(h):
                            def step(t, k):
                                t.wait(turned[h], k)
                                t.wait(z_up[h] if n == 0 else hid_up[h], k - 2)
                                act.activation(turned_s[k % 2][h][:, :], turned_p[h][:, :], ACT.Copy).then_inc(turned_in[h], 1)
                            return step

                        def relus(h):
                            def step(t, k):
                                t.wait(z_up[h], k)
                                t.wait(y_made, k - 1)
                                act.activation(relu[:, h, :, :], zp[h][:, :, 0:2 * D], ACT.Relu, scale=1.0 - SLOPE
                                               ).then_inc(relu_in[h], 1)
                            return step

                        def gelu_hidden(t, k):
                            for h in range(2):
                                t.wait(hid_up[h], k)
                            t.wait(out_up, k - 2)
                            act.activation(hid_s[k % 2][:, :], hid_p[k % 2][:, :], ACT.Gelu, bias=bu1[:, 0:1]
                                           ).then_inc(hid_in, 1)

                        def gelu_out(t, k):
                            t.wait(out_up, k)
                            t.wait_slot(stores, k - S, 16)
                            act.activation(flat(y[k % S][:, :, :]), out_p[k % 2][:, :], ACT.Gelu).then_inc(y_made, 1)

                        def square(t, k):
                            t.wait(y_made, k)
                            t.wait(ssq_in, k - 1)
                            act.activation(sq_a[:, :, :], y[k % S][:, :, :], ACT.Square).then_inc(squared, 1)

                        def square_centred(t, k):
                            t.wait(centred, k)
                            t.wait(var_in, k - 1)
                            act.activation(sq_b[:, :, :], y[k % S][:, :, :], ACT.Square, scale=D ** -0.5
                                           ).then_inc(squared2, 1)

                        def normalize_rows(t, k):
                            s = k % S
                            t.wait(rstd_ready, k)
                            t.wait(centred, k)
                            for g in range(GA):
                                last = act.activation(y[s][:, g, :], y[s][:, g, :], ACT.Copy, scale=small["rstd"][s][:, g:g + 1])
                            last.then_inc(normed_act, 1)

                        if n == 0:
                            run_steps(act, ((square, 2), (relus(1), 1), (square_centred, 4), (relus(0), 1),
                                            (turned_to_sbuf(0), 0), (turned_to_sbuf(1), -1), (normalize_rows, 5)),
                                      range(START - 5, START + S + 1), ())
                        else:
                            run_steps(act, ((gelu_hidden, 1), (turned_to_sbuf(0), 0), (square_centred, 4),
                                            (turned_to_sbuf(1), -1), (gelu_out, 1), (square, 1),
                                            (normalize_rows, 5)),
                                      range(START - 5, START + S + 1), ((1, 16),))

                    @block.vector
                    def _(dve):
                        def halves(h):
                            return slice(h * GH, (h + 1) * GH)

                        def first_add(h):
                            def step(t, k):
                                t.wait(relu_in[h], k)
                                t.wait_slot(stores, k - S, 16)
                                dve.tensor_tensor(y[k % S][:, halves(h), :], relu[:, h, :, 0:D], zp[h][:, :, 2 * D:3 * D], ALU.add
                                                  ).then_inc(half_added[h], 1)
                            return step

                        def second_add(t, k):
                            whole = y[k % S][:, :, :].rearrange("p (h g) f -> p h g f", h=2)
                            for h in range(2):
                                t.wait(half_added[h], k)
                            dve.tensor_tensor(whole, whole, relu[:, :, :, D:2 * D], ALU.add).then_inc(y_made, 1)

                        def sum_squares(t, k):
                            t.wait(squared, k)
                            dve.tensor_reduce(small["ssq"][k % S][:, :], sq_a[:, :, :], AX_X, ALU.add).then_inc(ssq_in, 1)

                        def guard_squares(t, k):
                            ssq = small["ssq"][k % S]
                            t.wait(ssq_in, k)
                            dve.tensor_scalar(ssq[:, :], ssq[:, :], L2_EPS, None, ALU.max).then_inc(ssq_ready, 1)

                        def scale(t, k):
                            s = k % S
                            t.wait(inv_ready, k)
                            dve.tensor_tensor(y[s][:, :, :], y[s][:, :, :], wide(small["inv"][s]), ALU.mult).then_inc(scaled, 1)

                        def add_rows(t, k):
                            s = k % S
                            t.wait(scaled, k)
                            dve.tensor_tensor(y[s][:, 0:GF, :], y[s][:, 0:GF, :], xs[s][:, 0:GF, :], ALU.add
                                              ).then_inc(added_dve, 1)

                        def mean(t, k):
                            s = k % S
                            t.wait(added, k)
                            t.wait(added_dve, k)
                            dve.tensor_reduce(small["mean"][s][:, :], y[s][:, :, :], AX_X, ALU.add).then_inc(mean_in, 1)

                        def centre(t, k):
                            s = k % S
                            t.wait(mean_in, k)
                            dve.scalar_tensor_tensor(out=y[s][:, :, :], in0=wide(small["mean"][s]), scalar=-1.0 / D,
                                                     in1=y[s][:, :, :], op0=ALU.mult, op1=ALU.add).then_inc(centred, 1)

                        def variance(t, k):
                            t.wait(squared2, k)
                            dve.tensor_reduce(small["var"][k % S][:, :], sq_b[:, :, :], AX_X, ALU.add).then_inc(var_in, 1)

                        def guard_variance(t, k):
                            var = small["var"][k % S]
                            t.wait(var_in, k)
                            dve.tensor_scalar(var[:, :], var[:, :], LN_EPS, None, ALU.add).then_inc(var_ready, 1)

                        def normalize(t, k):
                            s = k % S
                            t.wait(rstd_ready, k)
                            dve.tensor_tensor(y[s][:, GA:G, :], y[s][:, GA:G, :], wide(small["rstd"][s], GA), ALU.mult
                                              ).then_inc(normed, 1)

                        if n == 0:
                            run_steps(dve, ((second_add, 1), (scale, 2), (sum_squares, 1), (add_rows, 2), (normalize, 5), (first_add(1), 0),
                                            (guard_squares, 1), (variance, 3), (mean, 2), (guard_variance, 3),
                                            (first_add(0), 0), (centre, 2)),
                                      range(START - 5, START + S), ((1, 16), (2, 16)))
                        else:
                            run_steps(dve, ((centre, 3), (scale, 2), (guard_squares, 1), (normalize, 5), (add_rows, 2), (variance, 3),
                                            (mean, 2), (guard_variance, 3), (sum_squares, 0)),
                                      range(START - 5, START + S), ())

        edge_phase(0, x, agg[0])
        dense_phase(0)
        edge_phase(1, x1, agg[1])
        dense_phase(1)


_INS = ['x', 'src', 'dst', 'edge_weight', 'L0_gnn_W1', 'L0_gnn_W2', 'L0_gnn_b1', 'L0_gnn_b2', 'L1_gnn_W1p', 'L1_gnn_b1p',
        'L1_gnn_W2p', 'L1_gnn_b2p', 'L1_gnn_W1u', 'L1_gnn_b1u', 'L1_gnn_W2u', 'L1_gnn_b2u']


def kernel(**inputs):
    import numpy as _np
    import concourse.bacc as _bacc
    from concourse import mybir as _mybir
    from concourse.bass_utils import run_bass_kernel_spmd as _run

    nc = _bacc.Bacc("TRN2", target_bir_lowering=False, num_devices=1)
    arrays, args = {}, []
    for name in _INS:
        a = _np.ascontiguousarray(inputs[name])
        arrays[f"in_{name}"] = a
        args.append(nc.dram_tensor(f"in_{name}", a.shape, _mybir.dt.from_np(a.dtype), kind="ExternalInput").ap())
    args.append(nc.dram_tensor("out_0", arrays["in_x"].shape, _mybir.dt.float32, kind="ExternalOutput").ap())
    gnn_kernel(nc, *args)
    r = _run(nc, [arrays], core_ids=[0])
    return r.results[0]["out_0"]
```
